# Optimizing a Trainium2 kernel written in Bass

```python
import numpy as np
import jax
import jax.numpy as jnp

def _softmax(x, axis=-1):
    return jax.nn.softmax(x, axis=axis)

def _gelu(x):
    return jax.nn.gelu(x, approximate=True)

def _silu(x):
    return jax.nn.silu(x)

def _sigmoid(x):
    return jax.nn.sigmoid(x)

def _layernorm(x, axis=-1, eps=1e-05):
    m = jnp.mean(x, axis=axis, keepdims=True)
    v = jnp.var(x, axis=axis, keepdims=True)
    return (x - m) / jnp.sqrt(v + eps)

def _scatter_add(tgt, idx, src, axis=0):
    return tgt.at[idx].add(src)

def _segment_sum(src, seg, n):
    return jax.ops.segment_sum(src, seg, n)
kernel_name = 'mk_prb_d1_jaxref_r8_ebc6f1'

def setup_inputs(seed: int=0):
    np.random.seed(seed)
    _w = jnp.asarray

    def _L0_attn_setup():
        import math
        import jax, jax.numpy as jnp
        import numpy as np
        B, T, C, H, DQK, DV = (2, 256, 128, 16, 64, 64)
        key = jax.random.key(seed)
        ks = jax.random.split(key, 5)
        x = jax.random.normal(ks[0], (B, T, C), dtype=jnp.float32)
        w_q = jax.random.normal(ks[1], (H, DQK, C), dtype=jnp.float32) / math.sqrt(C)
        w_k = jax.random.normal(ks[2], (H, DQK, C), dtype=jnp.float32) / math.sqrt(C)
        w_v = jax.random.normal(ks[3], (H, DV, C), dtype=jnp.float32) / math.sqrt(C)
        w_o = jax.random.normal(ks[4], (DV * H, C), dtype=jnp.float32) / math.sqrt(C)
        return {'x': x, 'w_q': w_q, 'w_k': w_k, 'w_v': w_v, 'w_o': w_o}
    _L0_attn_in = _L0_attn_setup()

    def _L0_ffn_setup():
        import jax, jax.numpy as jnp
        import numpy as np
        D_MODEL = 128
        M = 64
        INNER = 16
        key = jax.random.key(seed)
        ks = jax.random.split(key, 9)

        def init(k, shape, fan_in):
            bound = 1.0 / np.sqrt(fan_in)
            return jax.random.uniform(k, shape, jnp.float32, -bound, bound)
        x = jax.random.normal(ks[0], (16, 512, D_MODEL), dtype=jnp.float32)
        Win = init(ks[1], (D_MODEL, M), D_MODEL)
        bin_ = init(ks[2], (M,), D_MODEL)
        W1 = init(ks[3], (M, INNER), 1)
        b1 = init(ks[4], (M, INNER), 1)
        W2 = init(ks[5], (M, INNER), INNER)
        b2 = init(ks[6], (M,), INNER)
        Wout = init(ks[7], (M, D_MODEL), M)
        bout = init(ks[8], (D_MODEL,), M)
        return {'x': x, 'Win': Win, 'bin_': bin_, 'W1': W1, 'b1': b1, 'W2': W2, 'b2': b2, 'Wout': Wout, 'bout': bout}
    _L0_ffn_in = _L0_ffn_setup()
    _d = {'L0_attn_x': _L0_attn_in['x'], 'L0_attn_w_q': _L0_attn_in['w_q'], 'L0_attn_w_k': _L0_attn_in['w_k'], 'L0_attn_w_v': _L0_attn_in['w_v'], 'L0_attn_w_o': _L0_attn_in['w_o'], 'L0_ffn_Win': _L0_ffn_in['Win'], 'L0_ffn_bin_': _L0_ffn_in['bin_'], 'L0_ffn_W1': _L0_ffn_in['W1'], 'L0_ffn_b1': _L0_ffn_in['b1'], 'L0_ffn_W2': _L0_ffn_in['W2'], 'L0_ffn_b2': _L0_ffn_in['b2'], 'L0_ffn_Wout': _L0_ffn_in['Wout'], 'L0_ffn_bout': _L0_ffn_in['bout']}
    _x0 = _d['L0_attn_x']
    _d['L0_attn_x'] = jax.random.normal(jax.random.fold_in(jax.random.key(seed), 1), (8, 512, 128), dtype=_x0.dtype)
    del _x0
    return _d

def reference(L0_attn_x, L0_attn_w_q, L0_attn_w_k, L0_attn_w_v, L0_attn_w_o, L0_ffn_Win, L0_ffn_bin_, L0_ffn_W1, L0_ffn_b1, L0_ffn_W2, L0_ffn_b2, L0_ffn_Wout, L0_ffn_bout):

    def _L0_attn_ref(x, w_q, w_k, w_v, w_o):
        import math
        import jax, jax.numpy as jnp
        import numpy as np
        B, T, C, H, DQK, DV = (2, 256, 128, 16, 64, 64)
        n, t, c = x.shape
        q = jnp.einsum('ntc,hdc->nhtd', x, w_q)
        k = jnp.einsum('ntc,hdc->nhtd', x, w_k)
        v = jnp.einsum('ntc,hdc->nhtd', x, w_v)
        scale = 1.0 / math.sqrt(w_q.shape[1])
        a = jnp.einsum('nhtd,nhsd->nhts', q, k) * scale
        causal = jnp.arange(t)[:, None] < jnp.arange(t)[None, :]
        a = jnp.where(causal[None, None, :, :], -jnp.inf, a)
        a = jax.nn.softmax(a, axis=3)
        y = jnp.einsum('nhts,nhsd->nthd', a, v).reshape(n, t, -1)
        return y @ w_o

    def _L0_ffn_ref(x, Win, bin_, W1, b1, W2, b2, Wout, bout):
        import jax, jax.numpy as jnp
        import numpy as np
        D_MODEL = 128
        M = 64
        INNER = 16
        s = jnp.einsum('btd,dm->btm', x, Win) + bin_
        h = jax.nn.relu(s[..., None] * W1 + b1)
        g = jnp.einsum('btmh,mh->btm', h, W2) + b2
        out = jnp.einsum('btm,md->btd', g, Wout) + bout
        return out
    x = L0_attn_x
    xn = _layernorm(x, axis=-1)
    x = x + _L0_attn_ref(xn, L0_attn_w_q, L0_attn_w_k, L0_attn_w_v, L0_attn_w_o) + _L0_ffn_ref(xn, L0_ffn_Win, L0_ffn_bin_, L0_ffn_W1, L0_ffn_b1, L0_ffn_W2, L0_ffn_b2, L0_ffn_Wout, L0_ffn_bout)
    return x

_drawn_inputs = setup_inputs


def setup_inputs(seed=0):
    import zlib

    import numpy as np

    out = dict(_drawn_inputs(seed))
    spreads = {}
    factors = {'L0_ffn_bin_': 8.0}
    for name, (base, spread) in spreads.items():
        noise = np.random.default_rng([zlib.crc32(name.encode()), seed]).standard_normal(out[name].shape)
        drawn = base * np.exp(spread * noise) if base else spread * noise
        out[name] = jnp.asarray(drawn.astype(out[name].dtype))
    for name, factor in factors.items():
        out[name] = (out[name] * factor).astype(out[name].dtype)
    return out
```

```python
import numpy as np
import concourse.bass as bass
from concourse import mybir
from contextlib import ExitStack



def transformer_block(nc, x, wqT, wkT, wvT, wo, w_in, b_in, w1, b1, w2, b2, w_out, b_out, out):
    f32, f16, bf16 = mybir.dt.float32, mybir.dt.float16, mybir.dt.bfloat16
    ALU, ACT, AX = mybir.AluOpType, mybir.ActivationFunctionType, mybir.AxisListType

    NB, T, C = x.shape
    D = 64
    HD = wqT.shape[1]
    M, INNER = w1.shape
    P = 128
    TT = T // P
    PAIRS = HD // P
    QUADS = PAIRS // 2
    CH = 5
    SCALE = float(D) ** -0.5
    EPS = 1e-5
    WS = 64.0
    MSC = 32.0
    LIFT = 8.0 * float(np.log(64.0))
    BIG = -1.0e30
    HALF = T // 2

    def col(h, j):
        return {0: h * 512, 1: 1024 + h * 512, 3: 1024 + h * 512 + 384, 2: 2048 + h * 256}[j]

    PARTS = [[(0, 0)], [(1, 0)], [(0, 1), (0, 3)], [(1, 1), (1, 3)], [(0, 2), (1, 2)]]

    def jobs_of(slot, place, first, last):
        found = []
        if slot == 4 and place == 0 and not last:
            found.append(("X", 0))
        if place == 0 and not (last and slot + 2 >= PAIRS):
            found.append(("M", slot + 2))
        if place == 1:
            if slot == 1 and not first:
                found.append(("O", 0))
            if slot == 0:
                found.append(("F", 0))
            if slot == 2 and not first:
                found.append(("R", 0))
            if slot == 0:
                found.append(("V", 2))
            if slot == 3:
                found.append(("V", 6))
        if place == 3 and not (first and slot == 0):
            found.append(("Y", slot - 1))
        late = slot == 4
        if not (last and slot + 4 >= PAIRS):
            if place == 2 + late:
                found.append(("Q", slot + 4))
            if place == 3 + late:
                found.append(("K", slot + 4))
        if place == 4:
            v = {0: 3, 1: 4, 2: 5, 3: 7}.get(slot)
            if v is not None:
                found.append(("V", v))
            if slot in (6, 7) and not last:
                found.append(("V", 8 + slot - 6))
        return found

    def ffn_at(slot, place):
        spots = [(s, c) for s in range(1, PAIRS) for c in ((2, 3, 4) if s < 3 else (2, 4))]
        return [u for u, spot in enumerate(spots) if spot == (slot, place)]

    PROLOGUE = [("X", 0), ("Q", 0), ("K", 0), ("Q", 1), ("K", 1), ("Q", 2), ("K", 2), ("Q", 3), ("K", 3),
                ("V", 0), ("V", 1), ("M", 0), ("M", 1)]
    EPILOGUE = [("Y", PAIRS - 1), ("O", 0), ("R", 0)]
    WITH_HI = "QKVX"

    def listing(first, last):
        return [j for s in range(PAIRS) for c in range(CH) for j in jobs_of(s, c, first, last)]

    N_FIRST, N_ALL = len(listing(True, False)), len(listing(False, False))
    HI_PRO = sum(k in WITH_HI for k, _ in PROLOGUE)
    HI_ALL = sum(k in WITH_HI for k, _ in listing(False, False))
    assert N_ALL % 2 == 0

    def job_base(n, first):
        return len(PROLOGUE) if first else N_ALL * n + (len(PROLOGUE) + N_FIRST - N_ALL)

    def hi_base(n):
        return HI_ALL * n + HI_PRO

    def numbered(n, first, last):
        table, k, h = {}, 0, 0
        for s in range(PAIRS):
            for c in range(CH):
                row = []
                for kind, which in jobs_of(s, c, first, last):
                    bank = (k + (len(PROLOGUE) if first else len(PROLOGUE) + N_FIRST - N_ALL)) % 2
                    row.append((kind, which, job_base(n, first) + k, hi_base(n) + h, bank))
                    k += 1
                    h += kind in WITH_HI
                table[s, c] = row
        return table

    def numbered_prologue():
        rows, h = [], 0
        for k, (kind, which) in enumerate(PROLOGUE):
            rows.append((kind, which, k, h, k % 2))
            h += kind in WITH_HI
        return rows

    def numbered_epilogue():
        k0 = job_base(NB - 1, False) + len(listing(False, True))
        return [(kind, which, k0 + k, 0, (k0 + k) % 2) for k, (kind, which) in enumerate(EPILOGUE)]

    def v_jobs_done(n, first, pair):
        quad = pair // 2
        if quad == 0:
            if first:
                return [i for i, j in enumerate(PROLOGUE) if j == ("V", 1)][0] + 1
            return job_base(n, False)
        k = listing(first, False).index(("V", 2 * quad + 1))
        return job_base(n, first) + k + 1

    ctx = ExitStack()
    with ctx:
        def sb(name, shape, dt):
            return ctx.enter_context(nc.sbuf_tensor(name, shape, dt))

        def pb(name):
            return ctx.enter_context(nc.psum_tensor(name, [P, 512], f32))

        def sem(name):
            return ctx.enter_context(nc.semaphore(name))

        w_raw = sb("w_raw", [P, 4, HD], f32)
        w_hi = sb("w_hi", [P, 4, HD], f16)
        w_lo = sb("w_lo", [P, 4, HD], f16)
        win_raw = sb("win_raw", [P, M], f32)
        win_hi = sb("win_hi", [P, M], f16)
        win_lo = sb("win_lo", [P, M], f16)
        wout_raw = sb("wout_raw", [P, C], f32)
        wout = sb("wout", [P, 2, C], f32)
        bout = sb("bout", [P, 1], f32)
        bin_ = sb("bin", [P, 1], f32)
        w1s = sb("w1s", [P, INNER], f32)
        b1s = sb("b1s", [P, INNER], f32)
        w2s = sb("w2s", [P, INNER], f32)
        b2s = sb("b2s", [P, 1], f32)
        id32 = sb("id32", [P, P], f32)
        id16 = sb("id16", [P, P], f16)
        idb = sb("idb", [P, P], bf16)
        maskb = sb("maskb", [P, P], bf16)
        xs = sb("xs", [P, NB * TT, C], f32)
        stats = sb("stats", [P, NB * TT, 6], f32)
        mv = sb("mv", [P, NB * TT, 2], f32)
        std = sb("std", [P, NB * TT], f32)
        rstd = sb("rstd", [P, NB * TT], f32)
        shift = sb("shift", [P, NB * TT], f32)
        xn = sb("xn", [P, TT, C], f32)
        xT_hi = sb("xT_hi", [P, T], f16)
        xT_lo = sb("xT_lo", [P, T], f16)
        qk_hi = sb("qk_hi", [P, 2, 2, T], f16)
        qk_lo = sb("qk_lo", [P, 2, 2, T], f16)
        SB = 4
        q_st = sb("q_st", [P, SB, 2, T], f16)
        k_st = sb("k_st", [P, SB, 2, T], f16)
        q_mx = sb("q_mx", [P, SB, 2, T], f16)
        k_mx = sb("k_mx", [P, SB, 2, T], f16)
        VW = D + 1
        v_hi = sb("v_hi", [P, QUADS, TT, 4, VW], f16)
        v_lo = sb("v_lo", [P, QUADS, TT, 4, D], f16)
        mx = sb("mx", [P, 2, 2 * TT], f32)
        mx16 = sb("mx16", [P, 2, 2 * TT], f16)
        mrow = sb("mrow", [2 * TT, 2, P], f16)
        p32 = sb("p32", [P, 2, CH * 512], f32)
        p_hi = sb("p_hi", [P, 2, CH * 512], f16)
        p_lo = sb("p_lo", [P, 2, CH * 512], f16)
        rden = sb("rden", [P, 2, TT], f32)
        y32 = sb("y32", [P, 2, TT, P], f32)
        y_hi = sb("y_hi", [P, 2, TT, P], f16)
        y_lo = sb("y_lo", [P, 2, TT, P], f16)
        yT = sb("yT", [P, PAIRS, 2, T], f16)
        fs = sb("fs", [P, HALF], f32)
        ft = sb("ft", [P, HALF], f32)
        fr = sb("fr", [P, HALF], f32)
        fg = sb("fg", [P, HALF], f32)
        oT = sb("oT", [P, T], f32)
        res = sb("res", [P, TT, C], f32)

        job_bank = [pb("job0"), pb("job1")]
        score_bank = [pb("score0"), pb("score1")]
        approx_bank = [pb("approx0"), pb("approx1")]
        y_bank = [pb("y0"), pb("y1")]

        x_in = [sem(f"x_in{n}") for n in range(NB)]
        w_in_qk = sem("w_in_qk")
        w_in_vo = sem("w_in_vo")
        w_in_ffn = sem("w_in_ffn")
        consts = sem("consts")
        dve_consts = sem("dve_consts")
        stat_done = sem("stat_done")
        std_done = sem("std_done")
        w_hi_done = sem("w_hi_done")
        w_lo_done = sem("w_lo_done")
        xn_done = sem("xn_done")
        job_done = sem("job_done")
        hi_done = sem("hi_done")
        job_read = sem("job_read")
        stacked = [sem(f"stacked{s}") for s in range(SB)]
        mrow_in = [sem(f"mrow_in{s}") for s in range(SB)]
        approx_done = sem("approx_done")
        max_done = sem("max_done")
        mx16_done = sem("mx16_done")
        score_done = sem("score_done")
        exp_done = sem("exp_done")
        mask_done = sem("mask_done")
        p_hi_done = sem("p_hi_done")
        p_lo_done = sem("p_lo_done")
        pv_done = sem("pv_done")
        rden_done = sem("rden_done")
        y32_done = sem("y32_done")
        y_hi_done = sem("y_hi_done")
        y_lo_done = sem("y_lo_done")
        ffn_step = sem("ffn_step")
        pool_on = sem("pool_on")
        sp_on = sem("sp_on")
        out_in = sem("out_in")
        FFN_STEPS = 3 * INNER

        block = ctx.enter_context(nc.Block())

        def batches(eng, prologue, body, epilogue):
            prologue()
            body(0, True, False)
            with eng.Fori(1, NB - 1) as n:
                body(n, False, False)
            body(NB - 1, False, True)
            epilogue()

        def uses(n, p):
            return (PAIRS // SB) * n + p // SB + 1

        def positive(v):
            return not isinstance(v, int) or v > 0

        @block.sync
        def _(sp):
            for n in range(NB):
                sp.dma_start(xs[:, n * TT:(n + 1) * TT, :], x[n].rearrange("(i p) c -> p i c", p=P)).then_inc(x_in[n], 16)
                if n == 0:
                    sp.dma_start(w_raw[:, 0, :], wqT).then_inc(w_in_qk, 16)
                    sp.dma_start(w_raw[:, 1, :], wkT).then_inc(w_in_qk, 16)

            def stack(g, p, done):
                b, s = p % 2, p % SB
                sp.wait_ge(job_read, done)
                sp.sem_inc(sp_on, 1)
                if positive(g - SB + 1):
                    sp.wait_ge(score_done, CH * (g - SB + 1))
                    sp.sem_inc(sp_on, 1)
                for h in range(2):
                    r = slice(h * D, (h + 1) * D)
                    sp.dma_start(q_st[0:D, s, h, :], qk_hi[r, b, 0, :]).then_inc(stacked[s], 16)
                    sp.dma_start(q_st[D:P, s, h, :], qk_lo[r, b, 0, :]).then_inc(stacked[s], 16)
                    sp.dma_start(k_st[0:D, s, h, :], qk_hi[r, b, 1, :]).then_inc(stacked[s], 16)
                    sp.dma_start(k_st[D:P, s, h, :], qk_hi[r, b, 1, :]).then_inc(stacked[s], 16)
                    sp.dma_start(q_mx[0:D, s, h, :], qk_hi[r, b, 0, :]).then_inc(stacked[s], 16)
                    sp.dma_start(k_mx[0:D, s, h, :], qk_lo[r, b, 1, :]).then_inc(stacked[s], 16)

            def maxima(g, p, done):
                sp.wait_ge(job_read, done)
                sp.sem_inc(sp_on, 1)
                if positive(g - SB + 1):
                    sp.wait_ge(score_done, CH * (g - SB + 1))
                    sp.sem_inc(sp_on, 1)
                sp.dma_start(q_mx[D:D + 1, p % SB, :, :].rearrange("o h (i t) -> o (h i) t", t=P),
                             mrow[:, p % 2, :]).then_inc(mrow_in[p % SB], 16)

            def prologue():
                for kind, which, k, _, _ in numbered_prologue():
                    if kind == "K":
                        stack(which, which, k + 1)
                    if kind == "M":
                        maxima(which, which, k + 1)

            def body(n, first, last):
                table = numbered(n, first, last)
                before = n - 1 if isinstance(n, int) else sp.snap(n - 1)
                for slot in range(PAIRS):
                    for c in range(CH):
                        for kind, which, k, _, _ in table[slot, c]:
                            if kind == "K":
                                stack(PAIRS * n + which, which, k + 1)
                            if kind == "M":
                                maxima(PAIRS * n + which, which, k + 1)
                            if kind == "R":
                                sp.wait_ge(job_read, k + 1)
                                sp.sem_inc(sp_on, 1)
                                sp.dma_start(out[bass.ds(before, 1)].rearrange("o (i p) c -> p (o i) c", p=P), res[:, :, :]).then_inc(out_in, 16)

            def epilogue():
                for kind, which, k, _, _ in numbered_epilogue():
                    if kind == "R":
                        sp.wait_ge(job_read, k + 1)
                        sp.sem_inc(sp_on, 1)
                        sp.dma_start(out[NB - 1].rearrange("(i p) c -> p i c", p=P), res[:, :, :]).then_inc(out_in, 16)
                sp.wait_ge(out_in, 16 * NB)

            batches(sp, prologue, body, epilogue)

        @block.gpsimd
        def _(pool):
            for m in (id32, id16, idb, maskb):
                pool.memset(m[:, :], 0.0).then_inc(consts, 1)
            pool.wait_ge(consts, 4)
            for m in (id32, id16, idb):
                pool.affine_select(out=m[:, :], in_=m[:, :], compare_op=ALU.not_equal, fill=1.0, base=0,
                                   pattern=[[-1, P]], channel_multiplier=1).then_inc(consts, 1)
            pool.affine_select(out=maskb[:, :], in_=maskb[:, :], compare_op=ALU.is_ge, fill=BIG, base=0,
                               pattern=[[-1, P]], channel_multiplier=1).then_inc(consts, 1)

            def mask(g, p, c):
                pool.wait_ge(exp_done, CH * g + c + 1)
                pool.sem_inc(pool_on, 1)
                for m, (h, j) in enumerate(PARTS[c]):
                    blk = p32[:, p % 2, col(h, j):col(h, j) + P]
                    last = pool.affine_select(out=blk, in_=blk, compare_op=ALU.is_ge, fill=0.0, base=0,
                                              pattern=[[1, P]], channel_multiplier=-1)
                last.then_inc(mask_done, 1)

            def part_y(g, p):
                b = p % 2
                pool.wait_ge(y32_done, 2 * g + 2)
                pool.sem_inc(pool_on, 1)
                pool.tensor_copy(y_hi[:, b], y32[:, b]).then_inc(y_hi_done, 1)
                pool.wait_ge(y_hi_done, g + 1)
                pool.sem_inc(pool_on, 1)
                pool.tensor_tensor(y_lo[:, b], y32[:, b], y_hi[:, b], ALU.subtract).then_inc(y_lo_done, 1)

            def ffn(n, u):
                k = FFN_STEPS * n + 3 * u
                if positive(k):
                    pool.wait_ge(ffn_step, k)
                    pool.sem_inc(pool_on, 1)
                pool.tensor_scalar(ft[:, :], fs[:, :], w1s[:, u:u + 1], b1s[:, u:u + 1], ALU.mult, ALU.add).then_inc(ffn_step, 1)
                pool.wait_ge(ffn_step, k + 1)
                pool.sem_inc(pool_on, 1)
                pool.tensor_scalar(fr[:, :], ft[:, :], 0.0, w2s[:, u:u + 1], ALU.max, ALU.mult).then_inc(ffn_step, 1)
                pool.wait_ge(ffn_step, k + 2)
                pool.sem_inc(pool_on, 1)
                if u == 0:
                    pool.tensor_scalar(fg[:, :], fr[:, :], 1.0, b2s[:, 0:1], ALU.mult, ALU.add).then_inc(ffn_step, 1)
                else:
                    pool.tensor_tensor(fg[:, :], fg[:, :], fr[:, :], ALU.add).then_inc(ffn_step, 1)

            def prologue():
                for c in range(CH):
                    mask(0, 0, c)

            def body(n, first, last):
                table = numbered(n, first, last)
                at = {kind: k for row in table.values() for kind, _, k, _, _ in row if kind in "FO"}
                f_job, o_job = at["F"], at.get("O")
                for slot in range(PAIRS):
                    if not (first and slot == 0):
                        part_y(PAIRS * n + slot - 1, slot - 1)
                    for c in range(CH):
                        if not (last and slot + 1 >= PAIRS):
                            mask(PAIRS * n + slot + 1, slot + 1, c)
                        for u in ffn_at(slot, c):
                            if u == 0:
                                pool.wait_ge(job_read, f_job + 1)
                                pool.sem_inc(pool_on, 1)
                                if not first:
                                    pool.wait_ge(job_done, o_job + 1)
                                    pool.sem_inc(pool_on, 1)
                            ffn(n, u)

            def epilogue():
                part_y(PAIRS * NB - 1, PAIRS - 1)

            batches(pool, prologue, body, epilogue)

        @block.scalar
        def _(act):
            act.dma_start(w_raw[:, 2, :], wvT).then_inc(w_in_vo, 16)
            act.dma_start(w_raw[:, 3, :].rearrange("p (g c) -> p g c", c=C), wo.rearrange("(g p) c -> p g c", p=P)).then_inc(w_in_vo, 16)
            act.dma_start(win_raw[:, :], w_in).then_inc(w_in_ffn, 16)
            for half in range(2):
                r = slice(half * M, (half + 1) * M)
                act.dma_start(wout_raw[r, :], w_out).then_inc(w_in_ffn, 16)
                act.dma_start(w1s[r, :], w1).then_inc(w_in_ffn, 16)
                act.dma_start(b1s[r, :], b1).then_inc(w_in_ffn, 16)
                act.dma_start(w2s[r, :], w2).then_inc(w_in_ffn, 16)
                act.dma_start(bin_[r, :], b_in.rearrange("(m o) -> m o", o=1)).then_inc(w_in_ffn, 16)
                act.dma_start(b2s[r, :], b2.rearrange("(m o) -> m o", o=1)).then_inc(w_in_ffn, 16)
            act.dma_start(bout[:, :], b_out.rearrange("(m o) -> m o", o=1)).then_inc(w_in_ffn, 16)
            act.wait_ge(w_in_qk, 32)
            for w in range(2):
                nc.scalar.activation(w_hi[:, w, :], w_raw[:, w, :], ACT.Copy, scale=WS).then_inc(w_hi_done, 1)
            act.wait_ge(w_in_vo, 32)
            for w in range(2, 4):
                nc.scalar.activation(w_hi[:, w, :], w_raw[:, w, :], ACT.Copy, scale=WS).then_inc(w_hi_done, 1)
            act.wait_ge(w_in_ffn, 16 * 14)
            nc.scalar.activation(win_hi[:, :], win_raw[:, :], ACT.Copy, scale=WS).then_inc(w_hi_done, 1)
            act.wait_ge(dve_consts, 3)
            for half in range(2):
                r = slice(half * M, (half + 1) * M)
                nc.scalar.activation(wout[r, half, :], wout_raw[r, :], ACT.Copy, scale=WS).then_inc(w_hi_done, 1)
            act.wait_ge(stat_done, NB * TT * 2 + 1)
            nc.scalar.activation(std[:, :], std[:, :], ACT.Sqrt).then_inc(std_done, 1)

            def high(n, kind, which, k, h, bank):
                if kind not in WITH_HI:
                    return
                src = job_bank[bank]
                g = PAIRS * n + which
                act.wait_ge(job_done, k + 1)
                if kind == "X":
                    nc.scalar.activation(xT_hi[:, :], src[:, :], ACT.Copy).then_inc(hi_done, 1)
                elif kind == "V":
                    q, half = (which // 2) % QUADS, which % 2
                    for j in range(2):
                        last = nc.scalar.activation(v_hi[:, q, 2 * half + j, :, 0:D],
                                                    src[:, j * 256:(j + 1) * 256].rearrange("p (h d) -> p h d", d=D),
                                                    ACT.Copy, scale=1 / WS)
                    last.then_inc(hi_done, 1)
                else:
                    if positive(g - 1):
                        act.wait_ge(stacked[(which - 2) % SB], 192 * uses(n, which - 2))
                    nc.scalar.activation(qk_hi[:, which % 2, int(kind == "K"), :], src[:, :], ACT.Copy,
                                         scale=1 / WS).then_inc(hi_done, 1)

            def exp(g, p, c):
                act.wait_ge(score_done, CH * g + c + 1)
                if positive(g - 1):
                    act.wait_ge(p_lo_done, CH * (g - 2) + c + 1)
                nc.scalar.activation(p32[:, p % 2, c * 512:(c + 1) * 512], score_bank[(CH * p + c) % 2][:, :],
                                     ACT.Exp, scale=SCALE).then_inc(exp_done, 1)

            def p_high(g, p, c):
                act.wait_ge(mask_done, CH * g + c + 1)
                if positive(g - 1):
                    act.wait_ge(pv_done, 2 * (g - 1))
                nc.scalar.activation(p_hi[:, p % 2, c * 512:(c + 1) * 512], p32[:, p % 2, c * 512:(c + 1) * 512],
                                     ACT.Copy).then_inc(p_hi_done, 1)

            def prologue():
                for job in numbered_prologue():
                    high(0, *job)
                for c in range(CH):
                    exp(0, 0, c)
                    if c >= 1:
                        p_high(0, 0, c - 1)
                p_high(0, 0, CH - 1)

            def body(n, first, last):
                table = numbered(n, first, last)
                for slot in range(PAIRS):
                    g, p = PAIRS * n + slot + 1, slot + 1
                    run = not (last and p >= PAIRS)
                    for c in range(CH):
                        for job in table[slot, c]:
                            high(n, *job)
                        if run:
                            exp(g, p, c)
                            if c >= 1:
                                p_high(g, p, c - 1)
                    if run:
                        p_high(g, p, CH - 1)

            batches(act, prologue, body, lambda: None)

        @block.vector
        def _(dve):
            V = nc.vector
            V.memset(k_mx[D:D + 1, :, :, :], MSC).then_inc(dve_consts, 1)
            V.memset(v_hi[:, :, :, :, D:VW], 1.0).then_inc(dve_consts, 1)
            V.memset(wout[:, :, :], 0.0).then_inc(dve_consts, 1)
            for t in range(NB * TT):
                if t % TT == 0:
                    dve.wait_ge(x_in[t // TT], 16)
                V.bn_stats(stats[:, t, :], xs[:, t, :]).then_inc(stat_done, 1)
            for t in range(NB * TT):
                dve.wait_ge(stat_done, NB * TT if t else NB * TT)
                V.bn_aggr(mv[:, t, :], stats[:, t, :]).then_inc(stat_done, 1)
            dve.wait_ge(stat_done, NB * TT * 2)
            V.tensor_scalar(std[:, :], mv[:, :, 1], EPS, None, ALU.add).then_inc(stat_done, 1)
            dve.wait_ge(std_done, 1)
            V.reciprocal(rstd[:, :], std[:, :]).then_inc(stat_done, 1)
            dve.wait_ge(stat_done, NB * TT * 2 + 2)
            V.tensor_tensor(shift[:, :], mv[:, :, 0], rstd[:, :], ALU.mult).then_inc(stat_done, 1)
            dve.wait_ge(stat_done, NB * TT * 2 + 3)
            V.tensor_scalar(shift[:, :], shift[:, :], -1.0, None, ALU.mult).then_inc(stat_done, 1)
            for w in range(4):
                dve.wait_ge(w_hi_done, w + 1)
                V.scalar_tensor_tensor(w_lo[:, w, :], w_raw[:, w, :], WS, w_hi[:, w, :], ALU.mult, ALU.subtract).then_inc(w_lo_done, 1)
            dve.wait_ge(w_hi_done, 5)
            V.scalar_tensor_tensor(win_lo[:, :], win_raw[:, :], WS, win_hi[:, :], ALU.mult, ALU.subtract).then_inc(w_lo_done, 1)

            def normalise(n):
                for i in range(TT):
                    t = n * TT + i
                    V.tensor_scalar(xn[:, i, :], xs[:, bass.ds(t, 1), :].rearrange("p o c -> p (o c)"),
                                    rstd[:, bass.ds(t, 1)], shift[:, bass.ds(t, 1)], ALU.mult, ALU.add).then_inc(xn_done, 1)

            dve.wait_ge(stat_done, NB * TT * 2 + 4)
            normalise(0)

            def read(n, kind, which, k, h, bank):
                src = job_bank[bank]
                dve.wait_ge(job_done, k + 1)
                if kind in WITH_HI:
                    dve.wait_ge(hi_done, h + 1)
                if kind == "X":
                    V.tensor_tensor(xT_lo[:, :], src[:, :], xT_hi[:, :], ALU.subtract).then_inc(job_read, 1)
                elif kind == "V":
                    q, half = (which // 2) % QUADS, which % 2
                    for j in range(2):
                        last = V.scalar_tensor_tensor(
                            v_lo[:, q, 2 * half + j, :, :], src[:, j * 256:(j + 1) * 256].rearrange("p (h d) -> p h d", d=D),
                            1 / WS, v_hi[:, q, 2 * half + j, :, 0:D], ALU.mult, ALU.subtract)
                    last.then_inc(job_read, 1)
                elif kind in "QK":
                    b, w = which % 2, int(kind == "K")
                    V.scalar_tensor_tensor(qk_lo[:, b, w, :], src[:, :], 1 / WS, qk_hi[:, b, w, :],
                                           ALU.mult, ALU.subtract).then_inc(job_read, 1)
                elif kind == "M":
                    if positive(PAIRS * n + which - 1):
                        dve.wait_ge(mrow_in[(which - 2) % SB], 16 * uses(n, which - 2))
                    V.tensor_copy(mrow[:, which % 2, :], src[0:2 * TT, 0:P // 2].bitcast(f16)).then_inc(job_read, 1)
                elif kind == "Y":
                    V.tensor_copy(yT[:, which % PAIRS, :, :].rearrange("p a t -> p (a t)"), src[:, :].bitcast(f16)).then_inc(job_read, 1)
                elif kind == "F":
                    if positive(n):
                        dve.wait_ge(ffn_step, FFN_STEPS * n)
                    V.tensor_scalar(fs[:, :], src[:, 0:HALF], 1 / WS, bin_[:, 0:1], ALU.mult, ALU.add).then_inc(job_read, 1)
                elif kind == "O":
                    V.tensor_scalar(oT[:, :], src[:, :], 1 / WS, bout[:, 0:1], ALU.mult, ALU.add).then_inc(job_read, 1)
                elif kind == "R":
                    m = n - 1
                    if positive(m):
                        dve.wait_ge(out_in, 16 * m)
                    V.tensor_tensor(res[:, :, :], src[:, :].rearrange("p (i c) -> p i c", c=C),
                                    xs[:, bass.ds(m * TT, TT), :], ALU.add).then_inc(job_read, 1)

            def maxes(g, p, c):
                src, b = approx_bank[(CH * p + c) % 2], p % 2
                dve.wait_ge(approx_done, CH * g + c + 1)
                if c < 4:
                    h = c % 2
                    if c < 2:
                        last = V.reduce_max(mx[:, b, h * TT + 3:h * TT + 4], src[:, :], AX.X)
                    else:
                        V.reduce_max(mx[:, b, h * TT + 2:h * TT + 3], src[:, 0:384], AX.X)
                        last = V.reduce_max(mx[:, b, h * TT:h * TT + 1], src[:, 384:512], AX.X)
                    last.then_inc(max_done, 1)
                else:
                    V.reduce_max(mx[:, b, 1:2 * TT:TT], src[:, :].rearrange("p (h s) -> p h s", h=2), AX.X).then_inc(max_done, 1)
                    dve.wait_ge(max_done, CH * g + CH)
                    V.tensor_scalar(mx16[:, b, :], mx[:, b, :], -1 / MSC, LIFT / MSC, ALU.mult, ALU.add).then_inc(mx16_done, 1)

            def p_low(g, p, c):
                s = slice(c * 512, (c + 1) * 512)
                dve.wait_ge(p_hi_done, CH * g + c + 1)
                V.tensor_tensor(p_lo[:, p % 2, s], p32[:, p % 2, s], p_hi[:, p % 2, s], ALU.subtract).then_inc(p_lo_done, 1)

            def y_norm(g, p, h):
                src, b = y_bank[h][:, 0:TT * VW].rearrange("p (i d) -> p i d", d=VW), p % 2
                dve.wait_ge(pv_done, 2 * g + h + 1)
                if positive(g - 1):
                    dve.wait_ge(y_lo_done, g - 1)
                V.reciprocal(rden[:, h, :], src[:, :, D]).then_inc(rden_done, 1)
                dve.wait_ge(rden_done, 2 * g + h + 1)
                V.tensor_tensor(y32[:, b, :, h * D:(h + 1) * D], src[:, :, 0:D],
                                rden[:, h, :].unsqueeze(2).broadcast_to([P, TT, D]), ALU.mult).then_inc(y32_done, 1)

            def prologue():
                jobs = numbered_prologue()
                for job in jobs[:-2]:
                    read(0, *job)
                for p in range(3):
                    for c in range(CH):
                        maxes(p, p, c)
                    if p < 2:
                        read(0, *jobs[len(jobs) - 2 + p])
                for c in range(CH):
                    p_low(0, 0, c)

            def body(n, first, last):
                table = numbered(n, first, last)
                for slot in range(PAIRS):
                    if slot == 3 and not last:
                        normalise(n + 1)
                    for c in range(CH):
                        for job in table[slot, c]:
                            read(n, *job)
                        if not (last and slot + 3 >= PAIRS):
                            maxes(PAIRS * n + slot + 3, slot + 3, c)
                        if not (last and slot + 1 >= PAIRS) and c >= 1:
                            p_low(PAIRS * n + slot + 1, slot + 1, c - 1)
                        if c == 3:
                            y_norm(PAIRS * n + slot, slot, 0)
                    if not (last and slot + 1 >= PAIRS):
                        p_low(PAIRS * n + slot + 1, slot + 1, CH - 1)
                    y_norm(PAIRS * n + slot, slot, 1)

            def epilogue():
                for job in numbered_epilogue():
                    read(NB, *job)

            batches(dve, prologue, body, epilogue)

        @block.tensor
        def _(pe):
            def mm(o, l, r, start, stop):
                return nc.tensor.matmul(o, l, r, start=start, stop=stop)

            def three(o, lh, ll, rh, rl, start, stop):
                mm(o, lh, rh, start, False)
                mm(o, lh, rl, False, False)
                return mm(o, ll, rh, False, stop)

            def job(n, first, kind, which, k, h, bank):
                dst = job_bank[bank]
                if positive(k - 1):
                    pe.wait_ge(job_read, k - 1)
                if kind == "X":
                    pe.wait_ge(xn_done, (n + 1) * TT if not (isinstance(n, int) and n < 0) else TT)
                    for i in range(TT):
                        last = nc.tensor.transpose(dst[:, i * P:(i + 1) * P], xn[:, i, :], id32[:, :])
                elif kind in "QK":
                    pe.wait_ge(job_read, k)
                    w, s = int(kind == "K"), slice((which % PAIRS) * P, (which % PAIRS) * P + P)
                    last = three(dst[:, :], w_hi[:, w, s], w_lo[:, w, s], xT_hi[:, :], xT_lo[:, :], True, True)
                elif kind == "V":
                    q, half = (which // 2) % QUADS, which % 2
                    s = slice(q * 256, (q + 1) * 256)
                    for j in range(2):
                        t = slice((2 * half + j) * P, (2 * half + j + 1) * P)
                        last = three(dst[:, j * 256:(j + 1) * 256], xT_hi[:, t], xT_lo[:, t], w_hi[:, 2, s], w_lo[:, 2, s], True, True)
                elif kind == "F":
                    for half in range(2):
                        t = slice(half * HALF, (half + 1) * HALF)
                        last = three(dst[half * M:(half + 1) * M, 0:HALF], win_hi[:, :], win_lo[:, :], xT_hi[:, t], xT_lo[:, t], True, True)
                elif kind == "M":
                    g = PAIRS * n + which
                    pe.wait_ge(mx16_done, g + 1)
                    last = nc.tensor.transpose(dst[0:2 * TT, 0:P // 2].bitcast(f16), mx16[:, which % 2, :], id16[:, :])
                elif kind == "Y":
                    g = PAIRS * n + which
                    pe.wait_ge(y_lo_done, g + 1)
                    d16 = dst[:, :].bitcast(f16)
                    for a, part in enumerate((y_hi, y_lo)):
                        for i in range(TT):
                            at = (a * TT + i) * P
                            last = nc.tensor.transpose(d16[:, at:at + P], part[:, which % 2, i, :], id16[:, :])
                elif kind == "O":
                    pe.wait_ge(job_read, k)
                    pe.wait_ge(ffn_step, FFN_STEPS * n)
                    pe.wait_ge(w_hi_done, 7)
                    for p in range(PAIRS):
                        s = slice(p * C, (p + 1) * C)
                        three(dst[:, :], w_hi[:, 3, s], w_lo[:, 3, s], yT[:, p, 0, :], yT[:, p, 1, :], p == 0, False)
                    for half in range(2):
                        last = mm(dst[:, half * HALF:(half + 1) * HALF], wout[:, half, :], fg[:, :], False, half == 1)
                elif kind == "R":
                    pe.wait_ge(job_read, k)
                    for i in range(TT):
                        last = nc.tensor.transpose(dst[:, i * P:(i + 1) * P], oT[:, i * P:(i + 1) * P], id32[:, :])
                last.then_inc(job_done, 1)

            def approx(n, p, c):
                g = PAIRS * n + p
                if c == 0:
                    pe.wait_ge(stacked[p % SB], 192 * uses(n, p))
                if positive(CH * g + c - 1):
                    pe.wait_ge(max_done, CH * g + c - 1)
                dst, s4, at = approx_bank[(CH * p + c) % 2], p % SB, 0
                for h, j in PARTS[c]:
                    i = TT - 1 - j
                    w = (i + 1) * P
                    mm(dst[:, at:at + w], q_st[:, s4, h, i * P:(i + 1) * P], k_st[:, s4, h, 0:w], True, False)
                    last = mm(dst[:, at + i * P:at + w], idb[:, :], maskb[:, :], False, True)
                    at += w
                last.then_inc(approx_done, 1)

            def scores(n, p, c):
                g = PAIRS * n + p
                if c == 0:
                    pe.wait_ge(mrow_in[p % SB], 16 * uses(n, p))
                if positive(CH * g + c - 1):
                    pe.wait_ge(exp_done, CH * g + c - 1)
                dst, s4, at = score_bank[(CH * p + c) % 2], p % SB, 0
                for h, j in PARTS[c]:
                    w, s, t = T - j * P, slice(j * P, (j + 1) * P), slice(j * P, T)
                    mm(dst[:, at:at + w], k_st[:, s4, h, s], q_st[:, s4, h, t], True, False)
                    last = mm(dst[:, at:at + w], k_mx[0:D + 1, s4, h, s], q_mx[0:D + 1, s4, h, t], False, True)
                    at += w
                last.then_inc(score_done, 1)

            BLOCKS = [(h, i, j) for h in range(2) for i in range(TT) for j in range(i + 1)]

            def pv(n, first, g, p, part):
                if part == 0:
                    pe.wait_ge(p_lo_done, CH * (g + 1))
                    pe.wait_ge(job_read, v_jobs_done(n, first, p))
                q, b, per = p // 2, p % 2, len(BLOCKS) // CH
                for h, i, j in BLOCKS[part * per:(part + 1) * per]:
                    if i == 0 and positive(2 * g + h - 1):
                        pe.wait_ge(y32_done, 2 * g + h - 1)
                    hh = (p % 2) * 2 + h
                    s = slice(col(h, j) + (i - j) * P, col(h, j) + (i - j + 1) * P)
                    o = y_bank[h][:, i * VW:i * VW + VW]
                    mm(o, p_hi[:, b, s], v_hi[:, q, j, hh, :], j == 0, False)
                    mm(o[:, 0:D], p_hi[:, b, s], v_lo[:, q, j, hh, :], False, False)
                    last = mm(o, p_lo[:, b, s], v_hi[:, q, j, hh, :], False, j == i)
                    if (i, j) == (TT - 1, TT - 1):
                        last.then_inc(pv_done, 1)

            def prologue():
                jobs = numbered_prologue()
                pe.wait_ge(consts, 8)
                pe.wait_ge(dve_consts, 3)
                for j in jobs[:-2]:
                    if j[0] == "Q" and j[1] == 0:
                        pe.wait_ge(w_lo_done, 2)
                    if j[0] == "V" and j[1] == 0:
                        pe.wait_ge(w_lo_done, 5)
                    job(0, True, *j)
                for p in range(3):
                    for c in range(CH):
                        approx(0, p, c)
                    if p < 2:
                        job(0, True, *jobs[len(jobs) - 2 + p])
                for c in range(CH):
                    scores(0, 0, c)

            def body(n, first, last):
                table = numbered(n, first, last)
                for slot in range(PAIRS):
                    for c in range(CH):
                        if not (last and slot + 1 >= PAIRS):
                            scores(n, slot + 1, c)
                        for j in table[slot, c]:
                            if j[0] == "X":
                                job(n + 1, first, *j)
                            else:
                                job(n, first, *j)
                        if not (last and slot + 3 >= PAIRS):
                            approx(n, slot + 3, c)
                        pv(n, first, PAIRS * n + slot, slot, c)

            def epilogue():
                for j in numbered_epilogue():
                    if j[0] == "Y":
                        job(NB - 1, False, *j)
                    else:
                        job(NB, False, *j)

            batches(pe, prologue, body, epilogue)


_INS = ["x", "wqT", "wkT", "wvT", "wo", "w_in", "b_in", "w1", "b1", "w2", "b2", "w_out", "b_out"]


def kernel(L0_attn_x, L0_attn_w_q, L0_attn_w_k, L0_attn_w_v, L0_attn_w_o, L0_ffn_Win, L0_ffn_bin_, L0_ffn_W1,
           L0_ffn_b1, L0_ffn_W2, L0_ffn_b2, L0_ffn_Wout, L0_ffn_bout):
    import concourse.bacc as bacc
    from concourse import mybir as mb
    from concourse.bass_utils import run_bass_kernel_spmd

    def rows_to_columns(w):
        w = np.asarray(w)
        return np.ascontiguousarray(w.reshape(-1, w.shape[-1]).T)

    given = [np.asarray(L0_attn_x), rows_to_columns(L0_attn_w_q), rows_to_columns(L0_attn_w_k), rows_to_columns(L0_attn_w_v),
             np.asarray(L0_attn_w_o), np.asarray(L0_ffn_Win), np.asarray(L0_ffn_bin_), np.asarray(L0_ffn_W1),
             np.asarray(L0_ffn_b1), np.asarray(L0_ffn_W2), np.asarray(L0_ffn_b2), np.asarray(L0_ffn_Wout), np.asarray(L0_ffn_bout)]
    nc = bacc.Bacc("TRN2", target_bir_lowering=False, num_devices=1)
    arrays, args = {}, []
    for name, a in zip(_INS, given):
        a = np.ascontiguousarray(a)
        arrays[name + "_dram"] = a
        args.append(nc.dram_tensor(name + "_dram", a.shape, mb.dt.from_np(a.dtype), kind="ExternalInput").ap())
    out = nc.dram_tensor("out_dram", given[0].shape, mb.dt.float32, kind="ExternalOutput").ap()
    transformer_block(nc, *args, out)
    r = run_bass_kernel_spmd(nc, [arrays], core_ids=[0])
    return r.results[0]["out_dram"]
```

```python
import numpy as np
import concourse.bass as bass
from concourse import mybir
from contextlib import ExitStack



def transformer_block(nc, x, wqT, wkT, wvT, wo, w_in, b_in, w1, b1, w2, b2, w_out, b_out, out):
    f32, f16, bf16 = mybir.dt.float32, mybir.dt.float16, mybir.dt.bfloat16
    ALU, ACT, AX = mybir.AluOpType, mybir.ActivationFunctionType, mybir.AxisListType

    NB, T, C = x.shape
    D = 64
    HD = wqT.shape[1]
    M, INNER = w1.shape
    P = 128
    TT = T // P
    PAIRS = HD // P
    QUADS = PAIRS // 2
    CH = 5
    SCALE = float(D) ** -0.5
    EPS = 1e-5
    WS = 64.0
    MSC = 32.0
    LIFT = 8.0 * float(np.log(64.0))
    BIG = -1.0e30
    HALF = T // 2

    def col(h, j):
        return {0: h * 512, 1: 1024 + h * 512, 3: 1024 + h * 512 + 384, 2: 2048 + h * 256}[j]

    PARTS = [[(0, 0)], [(1, 0)], [(0, 1), (0, 3)], [(1, 1), (1, 3)], [(0, 2), (1, 2)]]

    def jobs_of(slot, place, first, last):
        found = []
        if place == 1 and not (last and slot + 2 >= PAIRS):
            found.append(("M", slot + 2))
        if place in (0, 1) and not (last and slot + 4 >= PAIRS):
            found.append(("QK"[place], slot + 4))
        if place == 1 and slot == 1 and not first:
            found.append(("O", 0))
        if place == 2 and slot == 0:
            found.append(("F", 0))
        if place == 3:
            v = {0: 2, 1: 4, 2: 5, 3: 6}.get(slot)
            if v is not None:
                found.append(("V", v))
            if slot in (6, 7) and not last:
                found.append(("V", 8 + slot - 6))
            if slot == 4 and not first:
                found.append(("R", 0))
        if place == 4:
            if slot in (0, 3):
                found.append(("V", {0: 3, 3: 7}[slot]))
            if slot == 3 and not last:
                found.append(("X", 0))
            if not (first and slot == 0):
                found.append(("Y", slot - 1))
        return found

    def ffn_at(slot, place):
        spots = [(s, c) for s in range(1, PAIRS) for c in ((2, 3, 4) if s < 3 else (2, 4))]
        return [u for u, spot in enumerate(spots) if spot == (slot, place)]

    PROLOGUE = [("X", 0), ("Q", 0), ("K", 0), ("Q", 1), ("K", 1), ("Q", 2), ("K", 2), ("Q", 3), ("K", 3),
                ("V", 0), ("V", 1), ("M", 0), ("M", 1)]
    EPILOGUE = [("Y", PAIRS - 1), ("O", 0), ("R", 0)]
    WITH_HI = "QKVX"

    def listing(first, last):
        return [j for s in range(PAIRS) for c in range(CH) for j in jobs_of(s, c, first, last)]

    N_FIRST, N_ALL = len(listing(True, False)), len(listing(False, False))
    HI_PRO = sum(k in WITH_HI for k, _ in PROLOGUE)
    HI_ALL = sum(k in WITH_HI for k, _ in listing(False, False))
    assert N_ALL % 2 == 0

    def job_base(n, first):
        return len(PROLOGUE) if first else N_ALL * n + (len(PROLOGUE) + N_FIRST - N_ALL)

    def hi_base(n):
        return HI_ALL * n + HI_PRO

    def numbered(n, first, last):
        table, k, h = {}, 0, 0
        for s in range(PAIRS):
            for c in range(CH):
                row = []
                for kind, which in jobs_of(s, c, first, last):
                    bank = (k + (len(PROLOGUE) if first else len(PROLOGUE) + N_FIRST - N_ALL)) % 2
                    row.append((kind, which, job_base(n, first) + k, hi_base(n) + h, bank))
                    k += 1
                    h += kind in WITH_HI
                table[s, c] = row
        return table

    def numbered_prologue():
        rows, h = [], 0
        for k, (kind, which) in enumerate(PROLOGUE):
            rows.append((kind, which, k, h, k % 2))
            h += kind in WITH_HI
        return rows

    def numbered_epilogue():
        k0 = job_base(NB - 1, False) + len(listing(False, True))
        return [(kind, which, k0 + k, 0, (k0 + k) % 2) for k, (kind, which) in enumerate(EPILOGUE)]

    def v_jobs_done(n, first, pair):
        quad = pair // 2
        if quad == 0:
            if first:
                return [i for i, j in enumerate(PROLOGUE) if j == ("V", 1)][0] + 1
            return job_base(n, False) - 1
        k = listing(first, False).index(("V", 2 * quad + 1))
        return job_base(n, first) + k + 1

    ctx = ExitStack()
    with ctx:
        def sb(name, shape, dt):
            return ctx.enter_context(nc.sbuf_tensor(name, shape, dt))

        def pb(name):
            return ctx.enter_context(nc.psum_tensor(name, [P, 512], f32))

        def sem(name):
            return ctx.enter_context(nc.semaphore(name))

        w_raw = sb("w_raw", [P, 4, HD], f32)
        w_hi = sb("w_hi", [P, 4, HD], f16)
        w_lo = sb("w_lo", [P, 4, HD], f16)
        win_raw = sb("win_raw", [P, M], f32)
        win_hi = sb("win_hi", [P, M], f16)
        win_lo = sb("win_lo", [P, M], f16)
        wout_raw = sb("wout_raw", [P, C], f32)
        wout = sb("wout", [P, 2, C], f32)
        bout = sb("bout", [P, 1], f32)
        bin_ = sb("bin", [P, 1], f32)
        w1s = sb("w1s", [P, INNER], f32)
        b1s = sb("b1s", [P, INNER], f32)
        w2s = sb("w2s", [P, INNER], f32)
        b2s = sb("b2s", [P, 1], f32)
        id32 = sb("id32", [P, P], f32)
        id16 = sb("id16", [P, P], f16)
        idb = sb("idb", [P, P], bf16)
        maskb = sb("maskb", [P, P], bf16)
        xs = sb("xs", [P, NB * TT, C], f32)
        stats = sb("stats", [P, NB * TT, 6], f32)
        mv = sb("mv", [P, NB * TT, 2], f32)
        std = sb("std", [P, NB * TT], f32)
        rstd = sb("rstd", [P, NB * TT], f32)
        shift = sb("shift", [P, NB * TT], f32)
        xn = sb("xn", [P, TT, C], f32)
        xT_hi = sb("xT_hi", [P, T], f16)
        xT_lo = sb("xT_lo", [P, T], f16)
        KH, QH, KL, QL = range(4)
        qk = sb("qk", [P, 2, 4, T], f16)
        SB = 4
        K_ST, Q_ST, Q_MX, K_MX = range(4)
        stack = sb("stack", [P, SB, 4, 2, T], f16)
        VW = D + 1
        v_hi = sb("v_hi", [P, QUADS, TT, 4, VW], f16)
        v_lo = sb("v_lo", [P, QUADS, TT, 4, D], f16)
        mx = sb("mx", [P, 2, 2 * TT], f32)
        mx16 = sb("mx16", [P, 2, 2 * TT], f16)
        mrow = sb("mrow", [2 * TT, 2, P], f16)
        p32 = sb("p32", [P, 2, CH * 512], f32)
        p_hi = sb("p_hi", [P, 2, CH * 512], f16)
        p_lo = sb("p_lo", [P, 2, CH * 512], f16)
        rden = sb("rden", [P, 2, TT], f32)
        y32 = sb("y32", [P, 2, TT, P], f32)
        y_hi = sb("y_hi", [P, 2, TT, P], f16)
        y_lo = sb("y_lo", [P, 2, TT, P], f16)
        yT = sb("yT", [P, PAIRS, 2, T], f16)
        fs = sb("fs", [P, HALF], f32)
        ft = sb("ft", [P, HALF], f32)
        fr = sb("fr", [P, 2, HALF], f32)
        fg = sb("fg", [P, HALF], f32)
        oT = sb("oT", [P, T], f32)
        res = sb("res", [P, TT, C], f32)

        job_bank = [pb("job0"), pb("job1")]
        score_bank = [pb("score0"), pb("score1")]
        approx_bank = [pb("approx0"), pb("approx1")]
        y_bank = [pb("y0"), pb("y1")]

        x_in = [sem(f"x_in{n}") for n in range(NB)]
        w_in_qk = sem("w_in_qk")
        w_in_vo = sem("w_in_vo")
        w_in_ffn = sem("w_in_ffn")
        consts = sem("consts")
        dve_consts = sem("dve_consts")
        stat_done = sem("stat_done")
        std_done = sem("std_done")
        w_hi_done = sem("w_hi_done")
        w_lo_done = sem("w_lo_done")
        xn_done = sem("xn_done")
        job_done = sem("job_done")
        hi_done = sem("hi_done")
        job_read = sem("job_read")
        stacked = [sem(f"stacked{s}") for s in range(SB)]
        mrow_in = [sem(f"mrow_in{s}") for s in range(SB)]
        approx_done = sem("approx_done")
        max_done = sem("max_done")
        mx16_done = sem("mx16_done")
        score_done = sem("score_done")
        exp_done = sem("exp_done")
        mask_done = sem("mask_done")
        p_hi_done = sem("p_hi_done")
        p_lo_done = sem("p_lo_done")
        pv_done = sem("pv_done")
        rden_done = sem("rden_done")
        y32_done = sem("y32_done")
        y_hi_done = sem("y_hi_done")
        y_lo_done = sem("y_lo_done")
        yt_done = sem("yt_done")
        ffn_step = sem("ffn_step")
        pool_on = sem("pool_on")
        sp_on = sem("sp_on")
        out_in = sem("out_in")
        FFN_STEPS = 2 * INNER - 1
        relu_done = sem("relu_done")

        block = ctx.enter_context(nc.Block())

        def batches(eng, prologue, body, epilogue):
            prologue()
            body(0, True, False)
            with eng.Fori(1, NB - 1) as n:
                body(n, False, False)
            body(NB - 1, False, True)
            epilogue()

        def uses(n, p):
            return (PAIRS // SB) * n + p // SB + 1

        def positive(v):
            return not isinstance(v, int) or v > 0

        @block.sync
        def _(sp):
            for n in range(NB):
                sp.dma_start(xs[:, n * TT:(n + 1) * TT, :], x[n].rearrange("(i p) c -> p i c", p=P)).then_inc(x_in[n], 16)
                if n == 0:
                    sp.dma_start(w_raw[:, 0, :], wqT).then_inc(w_in_qk, 16)
                    sp.dma_start(w_raw[:, 1, :], wkT).then_inc(w_in_qk, 16)

            def stack_up(g, p, done):
                b, s = p % 2, p % SB
                sp.wait_ge(job_read, done)
                sp.sem_inc(sp_on, 1)
                if positive(g - SB + 1):
                    sp.wait_ge(score_done, CH * (g - SB + 1))
                    sp.sem_inc(sp_on, 1)
                for h in range(2):
                    r = slice(h * D, (h + 1) * D)
                    sp.dma_start(stack[0:D, s, K_ST:Q_ST + 1, h, :], qk[r, b, KH:QH + 1, :]).then_inc(stacked[s], 16)
                    sp.dma_start(stack[0:D, s, Q_MX:K_MX + 1, h, :], qk[r, b, QH:KL + 1, :]).then_inc(stacked[s], 16)
                    sp.dma_start(stack[D:P, s, K_ST:Q_ST + 1, h, :], qk[r, b, KH:QL + 1:3, :]).then_inc(stacked[s], 16)

            def maxima(g, p, done):
                sp.wait_ge(job_read, done)
                sp.sem_inc(sp_on, 1)
                if positive(g - SB + 1):
                    sp.wait_ge(score_done, CH * (g - SB + 1))
                    sp.sem_inc(sp_on, 1)
                sp.dma_start(stack[D:D + 1, p % SB, Q_MX, :, :].rearrange("o h (i t) -> o (h i) t", t=P),
                             mrow[:, p % 2, :]).then_inc(mrow_in[p % SB], 16)

            def prologue():
                for kind, which, k, _, _ in numbered_prologue():
                    if kind == "K":
                        stack_up(which, which, k + 1)
                    if kind == "M":
                        maxima(which, which, k + 1)

            def body(n, first, last):
                table = numbered(n, first, last)
                before = n - 1 if isinstance(n, int) else sp.snap(n - 1)
                for slot in range(PAIRS):
                    for c in range(CH):
                        for kind, which, k, _, _ in table[slot, c]:
                            if kind == "K":
                                stack_up(PAIRS * n + which, which, k + 1)
                            if kind == "M":
                                maxima(PAIRS * n + which, which, k + 1)
                            if kind == "R":
                                sp.wait_ge(job_read, k + 1)
                                sp.sem_inc(sp_on, 1)
                                sp.dma_start(out[bass.ds(before, 1)].rearrange("o (i p) c -> p (o i) c", p=P), res[:, :, :]).then_inc(out_in, 16)

            def epilogue():
                for kind, which, k, _, _ in numbered_epilogue():
                    if kind == "R":
                        sp.wait_ge(job_read, k + 1)
                        sp.sem_inc(sp_on, 1)
                        sp.dma_start(out[NB - 1].rearrange("(i p) c -> p i c", p=P), res[:, :, :]).then_inc(out_in, 16)
                sp.wait_ge(out_in, 16 * NB)

            batches(sp, prologue, body, epilogue)

        @block.gpsimd
        def _(pool):
            for m in (id32, id16, idb, maskb):
                pool.memset(m[:, :], 0.0).then_inc(consts, 1)
            pool.wait_ge(consts, 4)
            for m in (id32, id16, idb):
                pool.affine_select(out=m[:, :], in_=m[:, :], compare_op=ALU.not_equal, fill=1.0, base=0,
                                   pattern=[[-1, P]], channel_multiplier=1).then_inc(consts, 1)
            pool.affine_select(out=maskb[:, :], in_=maskb[:, :], compare_op=ALU.is_ge, fill=BIG, base=0,
                               pattern=[[-1, P]], channel_multiplier=1).then_inc(consts, 1)

            def mask(g, p, c):
                pool.wait_ge(exp_done, CH * g + c + 1)
                pool.sem_inc(pool_on, 1)
                for m, (h, j) in enumerate(PARTS[c]):
                    blk = p32[:, p % 2, col(h, j):col(h, j) + P]
                    last = pool.affine_select(out=blk, in_=blk, compare_op=ALU.is_ge, fill=0.0, base=0,
                                              pattern=[[1, P]], channel_multiplier=-1)
                last.then_inc(mask_done, 1)

            def y_low(g, p):
                b = p % 2
                pool.wait_ge(y_hi_done, g + 1)
                pool.sem_inc(pool_on, 1)
                pool.tensor_tensor(y_lo[:, b], y32[:, b], y_hi[:, b], ALU.subtract).then_inc(y_lo_done, 1)

            def ffn(n, u):
                k = FFN_STEPS * n + 2 * u - 1
                pool.wait_ge(relu_done, INNER * n + u + 1)
                pool.sem_inc(pool_on, 1)
                if u == 0:
                    pool.tensor_scalar(fg[:, :], fr[:, 0, :], w2s[:, 0:1], b2s[:, 0:1], ALU.mult, ALU.add).then_inc(ffn_step, 1)
                    return
                pool.wait_ge(ffn_step, k)
                pool.sem_inc(pool_on, 1)
                pool.tensor_scalar(ft[:, :], fr[:, u % 2, :], w2s[:, u:u + 1], 1.0, ALU.mult, ALU.mult).then_inc(ffn_step, 1)
                pool.wait_ge(ffn_step, k + 1)
                pool.sem_inc(pool_on, 1)
                pool.tensor_tensor(fg[:, :], fg[:, :], ft[:, :], ALU.add).then_inc(ffn_step, 1)

            def prologue():
                for c in range(CH):
                    mask(0, 0, c)

            def body(n, first, last):
                table = numbered(n, first, last)
                at = {kind: k for row in table.values() for kind, _, k, _, _ in row if kind in "FO"}
                o_job = at.get("O")
                for slot in range(PAIRS):
                    for c in range(CH):
                        if not (last and slot + 1 >= PAIRS):
                            mask(PAIRS * n + slot + 1, slot + 1, c)
                        for u in ffn_at(slot, c):
                            if u == 0 and not first:
                                    pool.wait_ge(job_done, o_job + 1)
                                    pool.sem_inc(pool_on, 1)
                            ffn(n, u)
                        if c == 1 and not (first and slot == 0):
                            y_low(PAIRS * n + slot - 1, slot - 1)

            def epilogue():
                y_low(PAIRS * NB - 1, PAIRS - 1)

            batches(pool, prologue, body, epilogue)

        @block.scalar
        def _(act):
            act.dma_start(w_raw[:, 2, :], wvT).then_inc(w_in_vo, 16)
            act.dma_start(w_raw[:, 3, :].rearrange("p (g c) -> p g c", c=C), wo.rearrange("(g p) c -> p g c", p=P)).then_inc(w_in_vo, 16)
            act.dma_start(win_raw[:, :], w_in).then_inc(w_in_ffn, 16)
            for half in range(2):
                r = slice(half * M, (half + 1) * M)
                act.dma_start(wout_raw[r, :], w_out).then_inc(w_in_ffn, 16)
                act.dma_start(w1s[r, :], w1).then_inc(w_in_ffn, 16)
                act.dma_start(b1s[r, :], b1).then_inc(w_in_ffn, 16)
                act.dma_start(w2s[r, :], w2).then_inc(w_in_ffn, 16)
                act.dma_start(bin_[r, :], b_in.rearrange("(m o) -> m o", o=1)).then_inc(w_in_ffn, 16)
                act.dma_start(b2s[r, :], b2.rearrange("(m o) -> m o", o=1)).then_inc(w_in_ffn, 16)
            act.dma_start(bout[:, :], b_out.rearrange("(m o) -> m o", o=1)).then_inc(w_in_ffn, 16)
            act.wait_ge(w_in_qk, 32)
            for w in range(2):
                nc.scalar.activation(w_hi[:, w, :], w_raw[:, w, :], ACT.Copy, scale=WS).then_inc(w_hi_done, 1)
            act.wait_ge(w_in_vo, 32)
            for w in range(2, 4):
                nc.scalar.activation(w_hi[:, w, :], w_raw[:, w, :], ACT.Copy, scale=WS).then_inc(w_hi_done, 1)
            act.wait_ge(w_in_ffn, 16 * 14)
            nc.scalar.activation(win_hi[:, :], win_raw[:, :], ACT.Copy, scale=WS).then_inc(w_hi_done, 1)
            act.wait_ge(dve_consts, 3)
            for half in range(2):
                r = slice(half * M, (half + 1) * M)
                nc.scalar.activation(wout[r, half, :], wout_raw[r, :], ACT.Copy, scale=WS).then_inc(w_hi_done, 1)
            act.wait_ge(stat_done, NB * TT * 2 + 1)
            nc.scalar.activation(std[:, :], std[:, :], ACT.Sqrt).then_inc(std_done, 1)

            def high(n, kind, which, k, h, bank):
                if kind not in WITH_HI:
                    return
                src = job_bank[bank]
                g = PAIRS * n + which
                act.wait_ge(job_done, k + 1)
                if kind == "X":
                    nc.scalar.activation(xT_hi[:, :], src[:, :], ACT.Copy).then_inc(hi_done, 1)
                elif kind == "V":
                    q, half = (which // 2) % QUADS, which % 2
                    for j in range(2):
                        last = nc.scalar.activation(v_hi[:, q, 2 * half + j, :, 0:D],
                                                    src[:, j * 256:(j + 1) * 256].rearrange("p (h d) -> p h d", d=D),
                                                    ACT.Copy, scale=1 / WS)
                    last.then_inc(hi_done, 1)
                else:
                    if positive(g - 1):
                        act.wait_ge(stacked[(which - 2) % SB], 96 * uses(n, which - 2))
                    nc.scalar.activation(qk[:, which % 2, QH if kind == "Q" else KH, :], src[:, :], ACT.Copy,
                                         scale=1 / WS).then_inc(hi_done, 1)

            def exp(g, p, c):
                act.wait_ge(score_done, CH * g + c + 1)
                if positive(g - 1):
                    act.wait_ge(p_lo_done, CH * (g - 2) + c + 1)
                nc.scalar.activation(p32[:, p % 2, c * 512:(c + 1) * 512], score_bank[(CH * p + c) % 2][:, :],
                                     ACT.Exp, scale=SCALE).then_inc(exp_done, 1)

            def p_high(g, p, c):
                act.wait_ge(mask_done, CH * g + c + 1)
                if positive(g - 1):
                    act.wait_ge(pv_done, 2 * (g - 1))
                nc.scalar.activation(p_hi[:, p % 2, c * 512:(c + 1) * 512], p32[:, p % 2, c * 512:(c + 1) * 512],
                                     ACT.Copy).then_inc(p_hi_done, 1)

            def y_high(g, p):
                act.wait_ge(y32_done, 2 * g + 2)
                if positive(2 * g - 3):
                    act.wait_ge(yt_done, g - 1)
                nc.scalar.activation(y_hi[:, p % 2], y32[:, p % 2], ACT.Copy).then_inc(y_hi_done, 1)

            def hidden(n, u, s_read):
                if s_read is not None:
                    act.wait_ge(job_read, s_read)
                if positive(FFN_STEPS * n + 2 * u - 3):
                    act.wait_ge(ffn_step, FFN_STEPS * n + 2 * u - 3 if u >= 2 else FFN_STEPS * n - 3 + 2 * u)
                nc.scalar.activation(fr[:, u % 2, :], fs[:, :], ACT.Relu, scale=w1s[:, u:u + 1],
                                     bias=b1s[:, u:u + 1]).then_inc(relu_done, 1)

            def prologue():
                for job in numbered_prologue():
                    high(0, *job)
                for c in range(CH):
                    exp(0, 0, c)
                    if c >= 1:
                        p_high(0, 0, c - 1)
                p_high(0, 0, CH - 1)

            def body(n, first, last):
                table = numbered(n, first, last)
                at = {(kind, which): k for row in table.values() for kind, which, k, _, _ in row}
                for slot in range(PAIRS):
                    g, p = PAIRS * n + slot + 1, slot + 1
                    run = not (last and p >= PAIRS)
                    for c in range(CH):
                        if run:
                            exp(g, p, c)
                        for job in table[slot, c]:
                            high(n, *job)
                        if run and c >= 1:
                            p_high(g, p, c - 1)
                        if c == 1 and not (first and slot == 0):
                            y_high(g - 2, p)
                        for u in ffn_at(slot, c):
                            hidden(n, u, at["F", 0] + 1 if u == 0 else None)
                    if run:
                        p_high(g, p, CH - 1)

            batches(act, prologue, body, lambda: y_high(PAIRS * NB - 1, 1))

        @block.vector
        def _(dve):
            V = nc.vector
            V.memset(stack[D:D + 1, :, K_MX, :, :], MSC).then_inc(dve_consts, 1)
            V.memset(v_hi[:, :, :, :, D:VW], 1.0).then_inc(dve_consts, 1)
            V.memset(wout[:, :, :], 0.0).then_inc(dve_consts, 1)
            for t in range(NB * TT):
                if t % TT == 0:
                    dve.wait_ge(x_in[t // TT], 16)
                V.bn_stats(stats[:, t, :], xs[:, t, :]).then_inc(stat_done, 1)
            for t in range(NB * TT):
                dve.wait_ge(stat_done, NB * TT if t else NB * TT)
                V.bn_aggr(mv[:, t, :], stats[:, t, :]).then_inc(stat_done, 1)
            dve.wait_ge(stat_done, NB * TT * 2)
            V.tensor_scalar(std[:, :], mv[:, :, 1], EPS, None, ALU.add).then_inc(stat_done, 1)
            dve.wait_ge(std_done, 1)
            V.reciprocal(rstd[:, :], std[:, :]).then_inc(stat_done, 1)
            dve.wait_ge(stat_done, NB * TT * 2 + 2)
            V.tensor_tensor(shift[:, :], mv[:, :, 0], rstd[:, :], ALU.mult).then_inc(stat_done, 1)
            dve.wait_ge(stat_done, NB * TT * 2 + 3)
            V.tensor_scalar(shift[:, :], shift[:, :], -1.0, None, ALU.mult).then_inc(stat_done, 1)
            for w in range(4):
                dve.wait_ge(w_hi_done, w + 1)
                V.scalar_tensor_tensor(w_lo[:, w, :], w_raw[:, w, :], WS, w_hi[:, w, :], ALU.mult, ALU.subtract).then_inc(w_lo_done, 1)
            dve.wait_ge(w_hi_done, 5)
            V.scalar_tensor_tensor(win_lo[:, :], win_raw[:, :], WS, win_hi[:, :], ALU.mult, ALU.subtract).then_inc(w_lo_done, 1)

            def normalise(n):
                for i in range(TT):
                    t = n * TT + i
                    V.tensor_scalar(xn[:, i, :], xs[:, bass.ds(t, 1), :].rearrange("p o c -> p (o c)"),
                                    rstd[:, bass.ds(t, 1)], shift[:, bass.ds(t, 1)], ALU.mult, ALU.add).then_inc(xn_done, 1)

            dve.wait_ge(stat_done, NB * TT * 2 + 4)
            normalise(0)

            def read(n, kind, which, k, h, bank):
                src = job_bank[bank]
                dve.wait_ge(job_done, k + 1)
                if kind in WITH_HI:
                    dve.wait_ge(hi_done, h + 1)
                if kind == "X":
                    V.tensor_tensor(xT_lo[:, :], src[:, :], xT_hi[:, :], ALU.subtract).then_inc(job_read, 1)
                elif kind == "V":
                    q, half = (which // 2) % QUADS, which % 2
                    for j in range(2):
                        last = V.scalar_tensor_tensor(
                            v_lo[:, q, 2 * half + j, :, :], src[:, j * 256:(j + 1) * 256].rearrange("p (h d) -> p h d", d=D),
                            1 / WS, v_hi[:, q, 2 * half + j, :, 0:D], ALU.mult, ALU.subtract)
                    last.then_inc(job_read, 1)
                elif kind in "QK":
                    b, (hi, lo) = which % 2, ((QH, QL) if kind == "Q" else (KH, KL))
                    V.scalar_tensor_tensor(qk[:, b, lo, :], src[:, :], 1 / WS, qk[:, b, hi, :],
                                           ALU.mult, ALU.subtract).then_inc(job_read, 1)
                elif kind == "M":
                    if positive(PAIRS * n + which - 1):
                        dve.wait_ge(mrow_in[(which - 2) % SB], 16 * uses(n, which - 2))
                    V.tensor_copy(mrow[:, which % 2, :], src[0:2 * TT, 0:P // 2].bitcast(f16)).then_inc(job_read, 1)
                elif kind == "Y":
                    V.tensor_copy(yT[:, which % PAIRS, :, :].rearrange("p a t -> p (a t)"), src[:, :].bitcast(f16)).then_inc(job_read, 1)
                elif kind == "F":
                    if positive(n):
                        dve.wait_ge(ffn_step, FFN_STEPS * n)
                    V.tensor_scalar(fs[:, :], src[:, 0:HALF], 1 / WS, bin_[:, 0:1], ALU.mult, ALU.add).then_inc(job_read, 1)
                elif kind == "O":
                    V.tensor_scalar(oT[:, :], src[:, :], 1 / WS, bout[:, 0:1], ALU.mult, ALU.add).then_inc(job_read, 1)
                elif kind == "R":
                    m = n - 1
                    if positive(m):
                        dve.wait_ge(out_in, 16 * m)
                    V.tensor_tensor(res[:, :, :], src[:, :].rearrange("p (i c) -> p i c", c=C),
                                    xs[:, bass.ds(m * TT, TT), :], ALU.add).then_inc(job_read, 1)

            def maxes(g, p, c):
                src, b = approx_bank[(CH * p + c) % 2], p % 2
                dve.wait_ge(approx_done, CH * g + c + 1)
                if c < 4:
                    h = c % 2
                    if c < 2:
                        last = V.reduce_max(mx[:, b, h * TT + 3:h * TT + 4], src[:, :], AX.X)
                    else:
                        V.reduce_max(mx[:, b, h * TT + 2:h * TT + 3], src[:, 0:384], AX.X)
                        last = V.reduce_max(mx[:, b, h * TT:h * TT + 1], src[:, 384:512], AX.X)
                    last.then_inc(max_done, 1)
                else:
                    V.reduce_max(mx[:, b, 1:2 * TT:TT], src[:, :].rearrange("p (h s) -> p h s", h=2), AX.X).then_inc(max_done, 1)
                    dve.wait_ge(max_done, CH * g + CH)
                    V.tensor_scalar(mx16[:, b, :], mx[:, b, :], -1 / MSC, LIFT / MSC, ALU.mult, ALU.add).then_inc(mx16_done, 1)

            def p_low(g, p, c):
                s = slice(c * 512, (c + 1) * 512)
                dve.wait_ge(p_hi_done, CH * g + c + 1)
                V.tensor_tensor(p_lo[:, p % 2, s], p32[:, p % 2, s], p_hi[:, p % 2, s], ALU.subtract).then_inc(p_lo_done, 1)

            def y_norm(g, p, h):
                src, b = y_bank[h][:, 0:TT * VW].rearrange("p (i d) -> p i d", d=VW), p % 2
                dve.wait_ge(pv_done, 2 * g + h + 1)
                if positive(g - 1):
                    dve.wait_ge(y_lo_done, g - 1)
                V.reciprocal(rden[:, h, :], src[:, :, D]).then_inc(rden_done, 1)
                dve.wait_ge(rden_done, 2 * g + h + 1)
                V.tensor_tensor(y32[:, b, :, h * D:(h + 1) * D], src[:, :, 0:D],
                                rden[:, h, :].unsqueeze(2).broadcast_to([P, TT, D]), ALU.mult).then_inc(y32_done, 1)

            def prologue():
                jobs = numbered_prologue()
                for job in jobs[:-2]:
                    read(0, *job)
                for p in range(3):
                    for c in range(CH):
                        maxes(p, p, c)
                    if p < 2:
                        read(0, *jobs[len(jobs) - 2 + p])
                for c in range(CH - 2):
                    p_low(0, 0, c)

            def body(n, first, last):
                table = numbered(n, first, last)
                for slot in range(PAIRS):
                    if slot == 3 and not last:
                        normalise(n + 1)
                    for c in range(CH):
                        if c == 0 and not (first and slot == 0):
                            y_norm(PAIRS * n + slot - 1, slot - 1, 1)
                        if c < 2:
                            p_low(PAIRS * n + slot, slot, c + 3)
                        elif not (last and slot + 1 >= PAIRS):
                            p_low(PAIRS * n + slot + 1, slot + 1, c - 2)
                        for job in table[slot, c]:
                            read(n, *job)
                        if not (last and slot + 3 >= PAIRS):
                            maxes(PAIRS * n + slot + 3, slot + 3, c)
                        if c == 4:
                            y_norm(PAIRS * n + slot, slot, 0)

            def epilogue():
                y_norm(PAIRS * NB - 1, PAIRS - 1, 1)
                for job in numbered_epilogue():
                    read(NB, *job)

            batches(dve, prologue, body, epilogue)

        @block.tensor
        def _(pe):
            def mm(o, l, r, start, stop):
                return nc.tensor.matmul(o, l, r, start=start, stop=stop)

            def three(o, lh, ll, rh, rl, start, stop):
                mm(o, lh, rh, start, False)
                mm(o, lh, rl, False, False)
                return mm(o, ll, rh, False, stop)

            def job(n, first, kind, which, k, h, bank, x_read=None, y_read=None, o_read=None):
                dst = job_bank[bank]
                if positive(k - 1):
                    pe.wait_ge(job_read, k - 1)
                if kind == "X":
                    pe.wait_ge(xn_done, (n + 1) * TT if not (isinstance(n, int) and n < 0) else TT)
                    for i in range(TT):
                        last = nc.tensor.transpose(dst[:, i * P:(i + 1) * P], xn[:, i, :], id32[:, :])
                elif kind in "QK":
                    if x_read is not None:
                        pe.wait_ge(job_read, x_read)
                    w, s = int(kind == "K"), slice((which % PAIRS) * P, (which % PAIRS) * P + P)
                    last = three(dst[:, :], w_hi[:, w, s], w_lo[:, w, s], xT_hi[:, :], xT_lo[:, :], True, True)
                elif kind == "V":
                    q, half = (which // 2) % QUADS, which % 2
                    s = slice(q * 256, (q + 1) * 256)
                    for j in range(2):
                        t = slice((2 * half + j) * P, (2 * half + j + 1) * P)
                        last = three(dst[:, j * 256:(j + 1) * 256], xT_hi[:, t], xT_lo[:, t], w_hi[:, 2, s], w_lo[:, 2, s], True, True)
                elif kind == "F":
                    for half in range(2):
                        t = slice(half * HALF, (half + 1) * HALF)
                        last = three(dst[half * M:(half + 1) * M, 0:HALF], win_hi[:, :], win_lo[:, :], xT_hi[:, t], xT_lo[:, t], True, True)
                elif kind == "M":
                    g = PAIRS * n + which
                    pe.wait_ge(mx16_done, g + 1)
                    last = nc.tensor.transpose(dst[0:2 * TT, 0:P // 2].bitcast(f16), mx16[:, which % 2, :], id16[:, :])
                elif kind == "Y":
                    g = PAIRS * n + which
                    pe.wait_ge(y_lo_done, g + 1)
                    d16 = dst[:, :].bitcast(f16)
                    for a, part in enumerate((y_hi, y_lo)):
                        for i in range(TT):
                            at = (a * TT + i) * P
                            last = nc.tensor.transpose(d16[:, at:at + P], part[:, which % 2, i, :], id16[:, :])
                        if a == 0:
                            last.then_inc(yt_done, 1)
                elif kind == "O":
                    pe.wait_ge(job_read, y_read)
                    pe.wait_ge(ffn_step, FFN_STEPS * n)
                    pe.wait_ge(w_hi_done, 7)
                    for p in range(PAIRS):
                        s = slice(p * C, (p + 1) * C)
                        three(dst[:, :], w_hi[:, 3, s], w_lo[:, 3, s], yT[:, p, 0, :], yT[:, p, 1, :], p == 0, False)
                    for half in range(2):
                        last = mm(dst[:, half * HALF:(half + 1) * HALF], wout[:, half, :], fg[:, :], False, half == 1)
                elif kind == "R":
                    pe.wait_ge(job_read, o_read)
                    for i in range(TT):
                        last = nc.tensor.transpose(dst[:, i * P:(i + 1) * P], oT[:, i * P:(i + 1) * P], id32[:, :])
                last.then_inc(job_done, 1)

            def approx(n, p, c):
                g = PAIRS * n + p
                if c == 0:
                    pe.wait_ge(stacked[p % SB], 96 * uses(n, p))
                if positive(CH * g + c - 1):
                    pe.wait_ge(max_done, CH * g + c - 1)
                dst, s4, at = approx_bank[(CH * p + c) % 2], p % SB, 0
                for h, j in PARTS[c]:
                    i = TT - 1 - j
                    w = (i + 1) * P
                    mm(dst[:, at:at + w], stack[:, s4, Q_ST, h, i * P:(i + 1) * P], stack[:, s4, K_ST, h, 0:w], True, False)
                    last = mm(dst[:, at + i * P:at + w], idb[:, :], maskb[:, :], False, True)
                    at += w
                last.then_inc(approx_done, 1)

            def scores(n, p, c):
                g = PAIRS * n + p
                if c == 0:
                    pe.wait_ge(mrow_in[p % SB], 16 * uses(n, p))
                if positive(CH * g + c - 1):
                    pe.wait_ge(exp_done, CH * g + c - 1)
                dst, s4, at = score_bank[(CH * p + c) % 2], p % SB, 0
                for h, j in PARTS[c]:
                    w, s, t = T - j * P, slice(j * P, (j + 1) * P), slice(j * P, T)
                    mm(dst[:, at:at + w], stack[:, s4, K_ST, h, s], stack[:, s4, Q_ST, h, t], True, False)
                    last = mm(dst[:, at:at + w], stack[0:D + 1, s4, K_MX, h, s], stack[0:D + 1, s4, Q_MX, h, t], False, True)
                    at += w
                last.then_inc(score_done, 1)

            BLOCKS = [(h, i, j) for rows in ((0, 1), (2, 3)) for h in range(2) for i in rows for j in range(i + 1)]

            def pv(n, first, g, p, part):
                if part == 0:
                    pe.wait_ge(p_lo_done, CH * g + 3)
                    pe.wait_ge(job_read, v_jobs_done(n, first, p))
                if part == 1:
                    pe.wait_ge(p_lo_done, CH * (g + 1))
                q, b, per = p // 2, p % 2, len(BLOCKS) // CH
                for h, i, j in BLOCKS[part * per:(part + 1) * per]:
                    if i == 0 and positive(2 * g + h - 1):
                        pe.wait_ge(y32_done, 2 * g + h - 1)
                    hh = (p % 2) * 2 + h
                    s = slice(col(h, j) + (i - j) * P, col(h, j) + (i - j + 1) * P)
                    o = y_bank[h][:, i * VW:i * VW + VW]
                    mm(o, p_hi[:, b, s], v_hi[:, q, j, hh, :], j == 0, False)
                    mm(o[:, 0:D], p_hi[:, b, s], v_lo[:, q, j, hh, :], False, False)
                    last = mm(o, p_lo[:, b, s], v_hi[:, q, j, hh, :], False, j == i)
                    if (i, j) == (TT - 1, TT - 1):
                        last.then_inc(pv_done, 1)

            def prologue():
                jobs = numbered_prologue()
                pe.wait_ge(consts, 8)
                pe.wait_ge(dve_consts, 3)
                for j in jobs[:-2]:
                    if j[0] == "Q" and j[1] == 0:
                        pe.wait_ge(w_lo_done, 2)
                    if j[0] == "V" and j[1] == 0:
                        pe.wait_ge(w_lo_done, 5)
                    job(0, True, *j, x_read=1 if j[:2] == ("Q", 0) else None)
                for p in range(3):
                    for c in range(CH):
                        approx(0, p, c)
                    if p < 2:
                        job(0, True, *jobs[len(jobs) - 2 + p])
                for c in range(CH):
                    scores(0, 0, c)

            def body(n, first, last):
                table = numbered(n, first, last)
                at = {(kind, which): k for row in table.values() for kind, which, k, _, _ in row}
                for slot in range(PAIRS):
                    for c in range(CH):
                        if not (last and slot + 1 >= PAIRS):
                            scores(n, slot + 1, c)
                        for j in table[slot, c]:
                            job(n + 1 if j[0] == "X" else n, first, *j,
                                x_read=at["X", 0] + 1 if j[:2] == ("Q", PAIRS) else None,
                                y_read=at["Y", -1] + 1 if j[0] == "O" else None,
                                o_read=at["O", 0] + 1 if j[0] == "R" else None)
                        if not (last and slot + 3 >= PAIRS):
                            approx(n, slot + 3, c)
                        pv(n, first, PAIRS * n + slot, slot, c)

            def epilogue():
                for j in numbered_epilogue():
                    job(NB - 1 if j[0] == "Y" else NB, False, *j, y_read=j[2], o_read=j[2])

            batches(pe, prologue, body, epilogue)


_INS = ["x", "wqT", "wkT", "wvT", "wo", "w_in", "b_in", "w1", "b1", "w2", "b2", "w_out", "b_out"]


def kernel(L0_attn_x, L0_attn_w_q, L0_attn_w_k, L0_attn_w_v, L0_attn_w_o, L0_ffn_Win, L0_ffn_bin_, L0_ffn_W1,
           L0_ffn_b1, L0_ffn_W2, L0_ffn_b2, L0_ffn_Wout, L0_ffn_bout):
    import concourse.bacc as bacc
    from concourse import mybir as mb
    from concourse.bass_utils import run_bass_kernel_spmd

    def rows_to_columns(w):
        w = np.asarray(w)
        return np.ascontiguousarray(w.reshape(-1, w.shape[-1]).T)

    given = [np.asarray(L0_attn_x), rows_to_columns(L0_attn_w_q), rows_to_columns(L0_attn_w_k), rows_to_columns(L0_attn_w_v),
             np.asarray(L0_attn_w_o), np.asarray(L0_ffn_Win), np.asarray(L0_ffn_bin_), np.asarray(L0_ffn_W1),
             np.asarray(L0_ffn_b1), np.asarray(L0_ffn_W2), np.asarray(L0_ffn_b2), np.asarray(L0_ffn_Wout), np.asarray(L0_ffn_bout)]
    nc = bacc.Bacc("TRN2", target_bir_lowering=False, num_devices=1)
    arrays, args = {}, []
    for name, a in zip(_INS, given):
        a = np.ascontiguousarray(a)
        arrays[name + "_dram"] = a
        args.append(nc.dram_tensor(name + "_dram", a.shape, mb.dt.from_np(a.dtype), kind="ExternalInput").ap())
    out = nc.dram_tensor("out_dram", given[0].shape, mb.dt.float32, kind="ExternalOutput").ap()
    transformer_block(nc, *args, out)
    r = run_bass_kernel_spmd(nc, [arrays], core_ids=[0])
    return r.results[0]["out_dram"]
```

```python
import numpy as np
import concourse.bass as bass
from concourse import mybir
from contextlib import ExitStack



def transformer_block(nc, x, wqT, wkT, wvT, wo, w_in, b_in, w1, b1, w2, b2, w_out, b_out, out):
    f32, f16, bf16 = mybir.dt.float32, mybir.dt.float16, mybir.dt.bfloat16
    ALU, ACT, AX = mybir.AluOpType, mybir.ActivationFunctionType, mybir.AxisListType

    NB, T, C = x.shape
    D = 64
    HD = wqT.shape[1]
    M, INNER = w1.shape
    P = 128
    TT = T // P
    PAIRS = HD // P
    QUADS = PAIRS // 2
    CH = 5
    SCALE = float(D) ** -0.5
    EPS = 1e-5
    WS = 64.0
    MSC = 32.0
    LIFT = 8.0 * float(np.log(64.0))
    BIG = -1.0e30
    HALF = T // 2

    def col(h, j):
        return {0: h * 512, 1: 1024 + h * 512, 3: 1024 + h * 512 + 384, 2: 2048 + h * 256}[j]

    PARTS = [[(0, 0)], [(1, 0)], [(0, 1), (0, 3)], [(1, 1), (1, 3)], [(0, 2), (1, 2)]]

    LOW_POOL, LOW_DVE = (1, 2, 3), (0, 4)

    O_PAIRS = [range(0, 3), range(3, 6), range(6, PAIRS)]

    def jobs_of(slot, place, first, last):
        found = []
        if place == 0 and not (last and slot + 4 >= PAIRS):
            found.append(("K", slot + 4))
        if place == 3 and not (first and slot == 0):
            found.append(("Y", slot - 1))
        if (slot, place) == (3, 2) and not last:
            found.append(("X", 0))
        v = {(0, 1): 4, (0, 2): 5, (2, 1): 6, (3, 1): 7, (4, 1): 8, (4, 2): 9, (5, 1): 10, (5, 2): 11}.get((slot, place))
        if v is not None and not (last and v >= 8):
            found.append(("V", v))
        if (slot, place) == (1, 2):
            found.append(("F", 0))
        o = {(6, 1): ("O", 0), (7, 1): ("O", 1), (1, 1): ("O", -1), (2, 2): ("R", 0)}.get((slot, place))
        if o is not None and not (first and slot < 3):
            found.append(o)
        if place == 4 and not (last and slot + 5 >= PAIRS):
            found.append(("Q", slot + 5))
        return found

    def ffn_at(slot, place):
        spots = [(1, 3), (1, 4)] + [(s, c) for s in range(2, PAIRS) for c in ((2, 3, 4) if s < 4 else (3, 4))]
        return [u for u, spot in enumerate(spots) if spot == (slot, place)]

    PROLOGUE = [("X", 0), ("Q", 0), ("K", 0), ("Q", 1), ("K", 1), ("Q", 2), ("K", 2), ("Q", 3), ("K", 3),
                ("V", 0), ("V", 1), ("V", 2), ("V", 3), ("Q", 4)]
    APPROX_READ = [("K", 1), ("K", 2), ("V", 1)]
    APPROX_MADE = [("K", 2), ("K", 3), ("V", 1)]
    EPILOGUE = [("Y", PAIRS - 1), ("O", -1), ("R", 0)]
    WITH_HI = "QKVX"

    def listing(first, last):
        return [j for s in range(PAIRS) for c in range(CH) for j in jobs_of(s, c, first, last)]

    N_FIRST, N_ALL = len(listing(True, False)), len(listing(False, False))
    HI_PRO = sum(k in WITH_HI for k, _ in PROLOGUE)
    HI_FIRST, HI_ALL = (sum(k in WITH_HI for k, _ in listing(first, False)) for first in (True, False))
    assert N_ALL % 2 == 0

    def job_base(n, first):
        return len(PROLOGUE) if first else N_ALL * n + (len(PROLOGUE) + N_FIRST - N_ALL)

    def hi_base(n, first):
        return HI_PRO if first else HI_ALL * n + (HI_PRO + HI_FIRST - HI_ALL)

    def numbered(n, first, last):
        table, k, h = {}, 0, 0
        for s in range(PAIRS):
            for c in range(CH):
                row = []
                for kind, which in jobs_of(s, c, first, last):
                    bank = (k + (len(PROLOGUE) if first else len(PROLOGUE) + N_FIRST - N_ALL)) % 2
                    row.append((kind, which, job_base(n, first) + k, hi_base(n, first) + h, bank))
                    k += 1
                    h += kind in WITH_HI
                table[s, c] = row
        return table

    def numbered_prologue():
        rows, h = [], 0
        for k, (kind, which) in enumerate(PROLOGUE):
            rows.append((kind, which, k, h, k % 2))
            h += kind in WITH_HI
        return rows

    def numbered_epilogue():
        k0 = job_base(NB - 1, False) + len(listing(False, True))
        return [(kind, which, k0 + k, 0, (k0 + k) % 2) for k, (kind, which) in enumerate(EPILOGUE)]

    def o_before(base, last):
        done = listing(False, last)
        return base - len(done) + done.index(("O", 1))

    def v_jobs_done(n, first, pair):
        quad = pair // 2
        v, own = ("V", 2 * quad + 1), listing(first, False)
        if first and v in PROLOGUE:
            return PROLOGUE.index(v) + 1
        if v in own:
            return job_base(n, first) + own.index(v) + 1
        before = listing(False, False)
        return job_base(n, False) - len(before) + before.index(("V", 2 * QUADS + 2 * quad + 1)) + 1

    ctx = ExitStack()
    with ctx:
        def sb(name, shape, dt):
            return ctx.enter_context(nc.sbuf_tensor(name, shape, dt))

        def pb(name):
            return ctx.enter_context(nc.psum_tensor(name, [P, 512], f32))

        def sem(name):
            return ctx.enter_context(nc.semaphore(name))

        w_raw = sb("w_raw", [P, 4, HD], f32)
        w_hi = sb("w_hi", [P, 4, HD], f16)
        w_lo = sb("w_lo", [P, 4, HD], f16)
        win_raw = sb("win_raw", [P, M], f32)
        win_hi = sb("win_hi", [P, M], f16)
        win_lo = sb("win_lo", [P, M], f16)
        wout_raw = sb("wout_raw", [P, C], f32)
        wout = sb("wout", [P, 2, C], f32)
        bout = sb("bout", [P, 1], f32)
        bin_ = sb("bin", [P, 1], f32)
        w1s = sb("w1s", [P, INNER], f32)
        b1s = sb("b1s", [P, INNER], f32)
        w2s = sb("w2s", [P, INNER], f32)
        b2s = sb("b2s", [P, 1], f32)
        id32 = sb("id32", [P, P], f32)
        id16 = sb("id16", [P, P], f16)
        idb = sb("idb", [P, P], bf16)
        maskb = sb("maskb", [P, P], bf16)
        maskT = sb("maskT", [P, P], bf16)
        xs = sb("xs", [P, NB * TT, C], f32)
        stats = sb("stats", [P, NB * TT, 6], f32)
        mv = sb("mv", [P, NB * TT, 2], f32)
        std = sb("std", [P, NB * TT], f32)
        rstd = sb("rstd", [P, NB * TT], f32)
        shift = sb("shift", [P, NB * TT], f32)
        xn = sb("xn", [P, TT, C], f32)
        xT_hi = sb("xT_hi", [P, T], f16)
        xT_lo = sb("xT_lo", [P, T], f16)
        KH, QH, KL, QL = range(4)
        qk = sb("qk", [P, 2, 4, T], f16)
        SB = 4
        K_ST, Q_ST, Q_MX, K_MX = range(4)
        stack = sb("stack", [P, SB, 4, 2, T], f16)
        VW = D + 1
        v_hi = sb("v_hi", [P, QUADS, TT, 4, VW], f16)
        v_lo = sb("v_lo", [P, QUADS, TT, 4, D], f16)
        mx = sb("mx", [P, 2, 2 * TT], f32)
        mx16 = sb("mx16", [P, 2, 2 * TT], f16)
        mrow = sb("mrow", [2 * TT, 2, P], f16)
        p32 = sb("p32", [P, 2, CH * 512], f32)
        p_hi = sb("p_hi", [P, 2, CH * 512], f16)
        p_lo = sb("p_lo", [P, 2, CH * 512], f16)
        rden = sb("rden", [P, 2, TT], f32)
        y32 = sb("y32", [P, 2, TT, P], f32)
        y_hi = sb("y_hi", [P, 2, TT, P], f16)
        y_lo = sb("y_lo", [P, 2, TT, P], f16)
        yT = sb("yT", [P, PAIRS, 2, T], f16)
        fs = sb("fs", [P, HALF], f32)
        ft = sb("ft", [P, HALF], f32)
        fr = sb("fr", [P, 2, HALF], f32)
        fg = sb("fg", [P, HALF], f32)
        oT = sb("oT", [P, T], f32)
        res = sb("res", [P, TT, C], f32)

        job_bank = [pb("job0"), pb("job1")]
        score_bank = [pb("score0"), pb("score1")]
        approx_bank = [pb("approx0"), pb("approx1")]
        y_bank = [pb("y0"), pb("y1")]

        def turned_to(p):
            return approx_bank[(CH * p + CH - 1) % 2][0:2 * TT, 0:P // 2].bitcast(f16)

        x_in = [sem(f"x_in{n}") for n in range(NB)]
        w_in_qk = sem("w_in_qk")
        w_in_vo = sem("w_in_vo")
        w_in_ffn = sem("w_in_ffn")
        consts = sem("consts")
        stat_done = sem("stat_done")
        std_done = sem("std_done")
        w_hi_done = sem("w_hi_done")
        w_lo_done = sem("w_lo_done")
        xn_done = sem("xn_done")
        job_done = sem("job_done")
        hi_done = sem("hi_done")
        job_read = sem("job_read")
        stacked = [sem(f"stacked{s}") for s in range(SB)]
        mrow_in = [sem(f"mrow_in{s}") for s in range(SB)]
        approx_done = sem("approx_done")
        max_done = sem("max_done")
        mx16_done = sem("mx16_done")
        turned = sem("turned")
        mrow_done = sem("mrow_done")
        score_done = sem("score_done")
        exp_done = sem("exp_done")
        p_hi_done = sem("p_hi_done")
        p_lo_done = sem("p_lo_done")
        p_lo_pool = sem("p_lo_pool")
        pv_done = sem("pv_done")
        rden_done = sem("rden_done")
        y32_done = sem("y32_done")
        y_hi_done = sem("y_hi_done")
        y_lo_done = sem("y_lo_done")
        yt_done = sem("yt_done")
        ffn_step = sem("ffn_step")
        pool_on = sem("pool_on")
        sp_on = sem("sp_on")
        out_in = sem("out_in")
        FFN_STEPS = 2 * INNER - 1
        relu_done = sem("relu_done")

        block = ctx.enter_context(nc.Block())

        def batches(eng, prologue, body, epilogue):
            prologue()
            body(0, True, False)
            with eng.Fori(1, NB - 1) as n:
                body(n, False, False)
            body(NB - 1, False, True)
            epilogue()

        def uses(n, p):
            return (PAIRS // SB) * n + p // SB + 1

        def positive(v):
            return not isinstance(v, int) or v > 0

        def low_there(g, c):
            if c in LOW_POOL:
                return p_lo_pool, len(LOW_POOL) * g + LOW_POOL.index(c) + 1
            return p_lo_done, len(LOW_DVE) * g + LOW_DVE.index(c) + 1

        def stat_steps(tiles):
            return 2 * tiles + 4

        @block.sync
        def _(sp):
            def load_x(n):
                sp.dma_start(xs[:, n * TT:(n + 1) * TT, :], x[n].rearrange("(i p) c -> p i c", p=P)).then_inc(x_in[n], 16)

            load_x(0)
            sp.dma_start(w_raw[:, 0, :], wqT).then_inc(w_in_qk, 16)
            sp.dma_start(w_raw[:, 1, :], wkT).then_inc(w_in_qk, 16)
            sp.dma_start(w_raw[:, 2, :], wvT).then_inc(w_in_vo, 16)
            sp.dma_start(w_raw[:, 3, :].rearrange("p (g c) -> p g c", c=C), wo.rearrange("(g p) c -> p g c", p=P)).then_inc(w_in_vo, 16)
            for n in range(1, NB):
                load_x(n)
            loads = [(win_raw[:, :], w_in), (bout[:, :], b_out.rearrange("(m o) -> m o", o=1))]
            for half in range(2):
                r = slice(half * M, (half + 1) * M)
                loads += [(wout_raw[r, :], w_out), (w1s[r, :], w1), (b1s[r, :], b1), (w2s[r, :], w2),
                          (bin_[r, :], b_in.rearrange("(m o) -> m o", o=1)), (b2s[r, :], b2.rearrange("(m o) -> m o", o=1))]
            for to, source in loads:
                sp.dma_start(to, source).then_inc(w_in_ffn, 16)

            def stack_up(g, p, done):
                b, s = p % 2, p % SB
                sp.wait_ge(job_read, done)
                sp.sem_inc(sp_on, 1)
                if positive(g - SB + 1):
                    sp.wait_ge(score_done, CH * (g - SB + 1))
                    sp.sem_inc(sp_on, 1)
                for h in range(2):
                    r = slice(h * D, (h + 1) * D)
                    sp.dma_start(stack[0:D, s, K_ST:Q_ST + 1, h, :], qk[r, b, KH:QH + 1, :]).then_inc(stacked[s], 16)
                    sp.dma_start(stack[0:D, s, Q_MX:K_MX + 1, h, :], qk[r, b, QH:KL + 1, :]).then_inc(stacked[s], 16)
                    sp.dma_start(stack[D:P, s, K_ST:Q_ST + 1, h, :], qk[r, b, KH:QL + 1:3, :]).then_inc(stacked[s], 16)

            def maxima(g, p):
                sp.wait_ge(mrow_done, g + 1)
                sp.sem_inc(sp_on, 1)
                if positive(g - SB + 1):
                    sp.wait_ge(score_done, CH * (g - SB + 1))
                    sp.sem_inc(sp_on, 1)
                sp.dma_start(stack[D:D + 1, p % SB, Q_MX, :, :].rearrange("o h (i t) -> o (h i) t", t=P),
                             mrow[:, p % 2, :]).then_inc(mrow_in[p % SB], 16)

            def prologue():
                for kind, which, k, _, _ in numbered_prologue():
                    if kind == "K":
                        if which >= 2:
                            maxima(which - 2, which - 2)
                        stack_up(which, which, k + 1)

            def body(n, first, last):
                table = numbered(n, first, last)
                before = n - 1 if isinstance(n, int) else sp.snap(n - 1)
                for slot in range(PAIRS):
                    if not (last and slot + 2 >= PAIRS):
                        maxima(PAIRS * n + slot + 2, slot + 2)
                    for c in range(CH):
                        for kind, which, k, _, _ in table[slot, c]:
                            if kind == "K":
                                stack_up(PAIRS * n + which, which, k + 1)
                            if kind == "R":
                                sp.wait_ge(job_read, k + 1)
                                sp.sem_inc(sp_on, 1)
                                sp.dma_start(out[bass.ds(before, 1)].rearrange("o (i p) c -> p (o i) c", p=P), res[:, :, :]).then_inc(out_in, 16)

            def epilogue():
                for kind, which, k, _, _ in numbered_epilogue():
                    if kind == "R":
                        sp.wait_ge(job_read, k + 1)
                        sp.sem_inc(sp_on, 1)
                        sp.dma_start(out[NB - 1].rearrange("(i p) c -> p i c", p=P), res[:, :, :]).then_inc(out_in, 16)
                sp.wait_ge(out_in, 16 * NB)

            batches(sp, prologue, body, epilogue)

        @block.gpsimd
        def _(pool):
            for m in (id32, id16, idb, maskb, maskT):
                pool.memset(m[:, :], 0.0).then_inc(consts, 1)
            pool.wait_ge(consts, 5)
            for m in (id32, id16, idb):
                pool.affine_select(out=m[:, :], in_=m[:, :], compare_op=ALU.not_equal, fill=1.0, base=0,
                                   pattern=[[-1, P]], channel_multiplier=1).then_inc(consts, 1)
            pool.affine_select(out=maskb[:, :], in_=maskb[:, :], compare_op=ALU.is_ge, fill=BIG, base=0,
                               pattern=[[-1, P]], channel_multiplier=1).then_inc(consts, 1)
            pool.affine_select(out=maskT[:, :], in_=maskT[:, :], compare_op=ALU.is_ge, fill=BIG, base=0,
                               pattern=[[1, P]], channel_multiplier=-1).then_inc(consts, 1)
            pool.memset(v_hi[:, :, :, :, D:VW], 1.0).then_inc(consts, 1)
            pool.memset(wout[:, :, :], 0.0).then_inc(consts, 1)
            pool.wait_ge(consts, 12)
            pool.memset(stack[D:D + 1, :, K_MX, :, :], MSC).then_inc(consts, 1)

            def p_low(g, p, c):
                s = slice(c * 512, (c + 1) * 512)
                pool.wait_ge(p_hi_done, CH * g + c + 1)
                pool.sem_inc(pool_on, 1)
                pool.tensor_tensor(p_lo[:, p % 2, s], p32[:, p % 2, s], p_hi[:, p % 2, s], ALU.subtract).then_inc(p_lo_pool, 1)

            def y_low(g, p):
                b = p % 2
                pool.wait_ge(y_hi_done, g + 1)
                pool.sem_inc(pool_on, 1)
                pool.tensor_tensor(y_lo[:, b], y32[:, b], y_hi[:, b], ALU.subtract).then_inc(y_lo_done, 1)

            def ffn(n, u):
                k = FFN_STEPS * n + 2 * u - 1
                pool.wait_ge(relu_done, INNER * n + u + 1)
                pool.sem_inc(pool_on, 1)
                if u == 0:
                    pool.tensor_scalar(fg[:, :], fr[:, 0, :], w2s[:, 0:1], b2s[:, 0:1], ALU.mult, ALU.add).then_inc(ffn_step, 1)
                    return
                pool.wait_ge(ffn_step, k)
                pool.sem_inc(pool_on, 1)
                pool.tensor_scalar(ft[:, :], fr[:, u % 2, :], w2s[:, u:u + 1], 1.0, ALU.mult, ALU.mult).then_inc(ffn_step, 1)
                pool.wait_ge(ffn_step, k + 1)
                pool.sem_inc(pool_on, 1)
                pool.tensor_tensor(fg[:, :], fg[:, :], ft[:, :], ALU.add).then_inc(ffn_step, 1)

            def prologue():
                for c in LOW_POOL:
                    if c < CH - 1:
                        p_low(0, 0, c)

            def body(n, first, last):
                table = numbered(n, first, last)
                at = {(kind, which): k for row in table.values() for kind, which, k, _, _ in row}
                for slot in range(PAIRS):
                    for c in range(CH):
                        if c == 0 and CH - 1 in LOW_POOL:
                            p_low(PAIRS * n + slot, slot, CH - 1)
                        if c - 1 in LOW_POOL and not (last and slot + 1 >= PAIRS):
                            p_low(PAIRS * n + slot + 1, slot + 1, c - 1)
                        for u in ffn_at(slot, c):
                            if u == 0 and not first:
                                pool.wait_ge(job_done, at["O", -1] + 1)
                                pool.sem_inc(pool_on, 1)
                            ffn(n, u)
                        if c == 1 and not (first and slot == 0):
                            y_low(PAIRS * n + slot - 1, slot - 1)

            def epilogue():
                y_low(PAIRS * NB - 1, PAIRS - 1)

            batches(pool, prologue, body, epilogue)

        @block.scalar
        def _(act):
            def weights_high(which, loaded, value):
                act.wait_ge(loaded, value)
                for w in which:
                    nc.scalar.activation(w_hi[:, w, :], w_raw[:, w, :], ACT.Copy, scale=WS).then_inc(w_hi_done, 1)

            def root(t0, t1, before):
                act.wait_ge(stat_done, before + 2 * (t1 - t0) + 1)
                nc.scalar.activation(std[:, t0:t1], std[:, t0:t1], ACT.Sqrt).then_inc(std_done, 1)

            def high(n, kind, which, k, h, bank):
                if kind not in WITH_HI:
                    return
                src = job_bank[bank]
                g = PAIRS * n + which
                act.wait_ge(job_done, k + 1)
                if kind == "X":
                    nc.scalar.activation(xT_hi[:, :], src[:, :], ACT.Copy).then_inc(hi_done, 1)
                elif kind == "V":
                    q, half = (which // 2) % QUADS, which % 2
                    for j in range(2):
                        last = nc.scalar.activation(v_hi[:, q, 2 * half + j, :, 0:D],
                                                    src[:, j * 256:(j + 1) * 256].rearrange("p (h d) -> p h d", d=D),
                                                    ACT.Copy, scale=1 / WS)
                    last.then_inc(hi_done, 1)
                else:
                    if positive(g - 1):
                        act.wait_ge(stacked[(which - 2) % SB], 96 * uses(n, which - 2))
                    nc.scalar.activation(qk[:, which % 2, QH if kind == "Q" else KH, :], src[:, :], ACT.Copy,
                                         scale=1 / WS).then_inc(hi_done, 1)

            def exp(g, p, c):
                act.wait_ge(score_done, CH * g + c + 1)
                if positive(g - 1):
                    act.wait_ge(*low_there(g - 2, c))
                nc.scalar.activation(p32[:, p % 2, c * 512:(c + 1) * 512], score_bank[(CH * p + c) % 2][:, :],
                                     ACT.Exp, scale=SCALE).then_inc(exp_done, 1)

            def p_high(g, p, c):
                act.wait_ge(exp_done, CH * g + c + 1)
                if positive(g - 1):
                    act.wait_ge(pv_done, 2 * (g - 1))
                nc.scalar.activation(p_hi[:, p % 2, c * 512:(c + 1) * 512], p32[:, p % 2, c * 512:(c + 1) * 512],
                                     ACT.Copy).then_inc(p_hi_done, 1)

            def y_high(g, p):
                act.wait_ge(y32_done, 2 * g + 2)
                if positive(2 * g - 3):
                    act.wait_ge(yt_done, g - 1)
                nc.scalar.activation(y_hi[:, p % 2], y32[:, p % 2], ACT.Copy).then_inc(y_hi_done, 1)

            def hidden(n, u, s_read):
                if s_read is not None:
                    act.wait_ge(job_read, s_read)
                if positive(FFN_STEPS * n + 2 * u - 3):
                    act.wait_ge(ffn_step, FFN_STEPS * n + 2 * u - 3)
                nc.scalar.activation(fr[:, u % 2, :], fs[:, :], ACT.Relu, scale=w1s[:, u:u + 1],
                                     bias=b1s[:, u:u + 1]).then_inc(relu_done, 1)

            def prologue():
                root(0, TT, 0)
                weights_high((0, 1), w_in_qk, 32)
                for job in numbered_prologue():
                    high(0, *job)
                    if job[:2] == ("K", 1):
                        weights_high((2, 3), w_in_vo, 32)
                        act.wait_ge(w_in_ffn, 16 * 14)
                        nc.scalar.activation(win_hi[:, :], win_raw[:, :], ACT.Copy, scale=WS).then_inc(w_hi_done, 1)
                        act.wait_ge(consts, 12)
                        for half in range(2):
                            r = slice(half * M, (half + 1) * M)
                            nc.scalar.activation(wout[r, half, :], wout_raw[r, :], ACT.Copy, scale=WS).then_inc(w_hi_done, 1)
                    if job[:2] == ("K", 3):
                        root(TT, NB * TT, stat_steps(TT))
                    if job[:2] == ("V", 1):
                        for c in range(2):
                            exp(0, 0, c)
                        p_high(0, 0, 0)
                for c in range(2, CH):
                    exp(0, 0, c)
                    p_high(0, 0, c - 1)
                p_high(0, 0, CH - 1)

            def body(n, first, last):
                table = numbered(n, first, last)
                at = {(kind, which): k for row in table.values() for kind, which, k, _, _ in row}
                for slot in range(PAIRS):
                    g, p = PAIRS * n + slot + 1, slot + 1
                    run = not (last and p >= PAIRS)
                    for c in range(CH):
                        if run and c >= 1:
                            p_high(g, p, c - 1)
                        if run:
                            exp(g, p, c)
                        for job in table[slot, c]:
                            high(n, *job)
                        if c == 1 and not (first and slot == 0):
                            y_high(g - 2, p)
                        for u in ffn_at(slot, c):
                            hidden(n, u, at["F", 0] + 1 if u == 0 else None)
                    if run:
                        p_high(g, p, CH - 1)

            batches(act, prologue, body, lambda: y_high(PAIRS * NB - 1, 1))

        @block.vector
        def _(dve):
            V = nc.vector

            def statistics(t0, t1):
                for t in range(t0, t1):
                    if t % TT == 0:
                        dve.wait_ge(x_in[t // TT], 16)
                    V.bn_stats(stats[:, t, :], xs[:, t, :]).then_inc(stat_done, 1)

            def variances(t0, t1, before):
                dve.wait_ge(stat_done, before + (t1 - t0))
                for t in range(t0, t1):
                    V.bn_aggr(mv[:, t, :], stats[:, t, :]).then_inc(stat_done, 1)
                dve.wait_ge(stat_done, before + 2 * (t1 - t0))
                V.tensor_scalar(std[:, t0:t1], mv[:, t0:t1, 1], EPS, None, ALU.add).then_inc(stat_done, 1)

            def inverses(t0, t1, before, roots):
                s, steps = slice(t0, t1), before + 2 * (t1 - t0) + 1
                dve.wait_ge(std_done, roots)
                V.reciprocal(rstd[:, s], std[:, s]).then_inc(stat_done, 1)
                dve.wait_ge(stat_done, steps + 1)
                V.tensor_tensor(shift[:, s], mv[:, s, 0], rstd[:, s], ALU.mult).then_inc(stat_done, 1)
                dve.wait_ge(stat_done, steps + 2)
                V.tensor_scalar(shift[:, s], shift[:, s], -1.0, None, ALU.mult).then_inc(stat_done, 1)
                dve.wait_ge(stat_done, steps + 3)

            def weights_low(which):
                for w in which:
                    dve.wait_ge(w_hi_done, w + 1)
                    V.scalar_tensor_tensor(w_lo[:, w, :], w_raw[:, w, :], WS, w_hi[:, w, :], ALU.mult, ALU.subtract).then_inc(w_lo_done, 1)

            def normalise(n):
                for i in range(TT):
                    t = n * TT + i
                    V.tensor_scalar(xn[:, i, :], xs[:, bass.ds(t, 1), :].rearrange("p o c -> p (o c)"),
                                    rstd[:, bass.ds(t, 1)], shift[:, bass.ds(t, 1)], ALU.mult, ALU.add).then_inc(xn_done, 1)

            def read(n, kind, which, k, h, bank, before=None):
                src = job_bank[bank]
                dve.wait_ge(job_done, k + 1)
                if kind in WITH_HI:
                    dve.wait_ge(hi_done, h + 1)
                if kind == "X":
                    V.tensor_tensor(xT_lo[:, :], src[:, :], xT_hi[:, :], ALU.subtract).then_inc(job_read, 1)
                elif kind == "V":
                    q, half = (which // 2) % QUADS, which % 2
                    for j in range(2):
                        last = V.scalar_tensor_tensor(
                            v_lo[:, q, 2 * half + j, :, :], src[:, j * 256:(j + 1) * 256].rearrange("p (h d) -> p h d", d=D),
                            1 / WS, v_hi[:, q, 2 * half + j, :, 0:D], ALU.mult, ALU.subtract)
                    last.then_inc(job_read, 1)
                elif kind in "QK":
                    b, (hi, lo) = which % 2, ((QH, QL) if kind == "Q" else (KH, KL))
                    V.scalar_tensor_tensor(qk[:, b, lo, :], src[:, :], 1 / WS, qk[:, b, hi, :],
                                           ALU.mult, ALU.subtract).then_inc(job_read, 1)
                elif kind == "Y":
                    V.tensor_copy(yT[:, which % PAIRS, :, :].rearrange("p a t -> p (a t)"), src[:, :].bitcast(f16)).then_inc(job_read, 1)
                elif kind == "F":
                    if positive(n):
                        dve.wait_ge(ffn_step, FFN_STEPS * n)
                    V.tensor_scalar(fs[:, :], src[:, 0:HALF], 1 / WS, bin_[:, 0:1], ALU.mult, ALU.add).then_inc(job_read, 1)
                elif kind == "O" and which:
                    dve.wait_ge(job_read, before)
                    V.scalar_tensor_tensor(oT[:, :], src[:, :], 1 / WS, oT[:, :], ALU.mult, ALU.add).then_inc(job_read, 1)
                elif kind == "O":
                    V.tensor_scalar(oT[:, :], src[:, :], 1 / WS, bout[:, 0:1], ALU.mult, ALU.add).then_inc(job_read, 1)
                elif kind == "R":
                    m = n - 1
                    if positive(m):
                        dve.wait_ge(out_in, 16 * m)
                    V.tensor_tensor(res[:, :, :], src[:, :].rearrange("p (i c) -> p i c", c=C),
                                    xs[:, bass.ds(m * TT, TT), :], ALU.add).then_inc(job_read, 1)

            def maxes(g, p, c):
                src, b = approx_bank[(CH * p + c) % 2], p % 2
                dve.wait_ge(approx_done, CH * g + c + 1)
                if c < 4:
                    h = c % 2
                    if c < 2:
                        last = V.reduce_max(mx[:, b, h * TT + 3:h * TT + 4], src[:, :], AX.X)
                    else:
                        V.reduce_max(mx[:, b, h * TT + 2:h * TT + 3], src[:, 0:384], AX.X)
                        last = V.reduce_max(mx[:, b, h * TT:h * TT + 1], src[:, 384:512], AX.X)
                    last.then_inc(max_done, 1)
                else:
                    V.reduce_max(mx[:, b, 1:2 * TT:TT], src[:, :].rearrange("p (h s) -> p h s", h=2), AX.X).then_inc(max_done, 1)
                    dve.wait_ge(max_done, CH * g + CH)
                    V.tensor_scalar(mx16[:, b, :], mx[:, b, :], -1 / MSC, LIFT / MSC, ALU.mult, ALU.add).then_inc(mx16_done, 1)

            def max_rows(n, p):
                g = PAIRS * n + p
                dve.wait_ge(turned, g + 1)
                if positive(g - 1):
                    dve.wait_ge(mrow_in[(p - 2) % SB], 16 * uses(n, p - 2))
                V.tensor_copy(mrow[:, p % 2, :], turned_to(p)).then_inc(mrow_done, 1)

            def p_low(g, p, c):
                s = slice(c * 512, (c + 1) * 512)
                dve.wait_ge(p_hi_done, CH * g + c + 1)
                V.tensor_tensor(p_lo[:, p % 2, s], p32[:, p % 2, s], p_hi[:, p % 2, s], ALU.subtract).then_inc(p_lo_done, 1)

            def y_norm(g, p, h):
                src, b = y_bank[h][:, 0:TT * VW].rearrange("p (i d) -> p i d", d=VW), p % 2
                dve.wait_ge(pv_done, 2 * g + h + 1)
                if positive(g - 1):
                    dve.wait_ge(y_lo_done, g - 1)
                V.reciprocal(rden[:, h, :], src[:, :, D]).then_inc(rden_done, 1)
                dve.wait_ge(rden_done, 2 * g + h + 1)
                V.tensor_tensor(y32[:, b, :, h * D:(h + 1) * D], src[:, :, 0:D],
                                rden[:, h, :].unsqueeze(2).broadcast_to([P, TT, D]), ALU.mult).then_inc(y32_done, 1)

            def prologue():
                rest, done = (TT, NB * TT), stat_steps(TT)
                statistics(0, TT)
                variances(0, TT, 0)
                inverses(0, TT, 0, 1)
                normalise(0)
                weights_low((0, 1))
                for job in numbered_prologue():
                    read(0, *job)
                    if job[:2] == ("K", 1):
                        statistics(*rest)
                    if job[:2] == ("K", 2):
                        weights_low((2, 3))
                        dve.wait_ge(w_hi_done, 5)
                        V.scalar_tensor_tensor(win_lo[:, :], win_raw[:, :], WS, win_hi[:, :], ALU.mult, ALU.subtract).then_inc(w_lo_done, 1)
                    if job[:2] in APPROX_READ:
                        p = APPROX_READ.index(job[:2])
                        for c in range(CH):
                            maxes(p, p, c)
                        if p < 2:
                            max_rows(0, p)
                        if p == 1:
                            variances(*rest, done)
                    if job[:2] == ("V", 0):
                        inverses(*rest, done, 2)
                for c in LOW_DVE:
                    if c < CH - 1:
                        p_low(0, 0, c)

            def body(n, first, last):
                table = numbered(n, first, last)
                at = {(kind, which): k for row in table.values() for kind, which, k, _, _ in row}
                for slot in range(PAIRS):
                    if slot == 1 and not last:
                        normalise(n + 1)
                    for c in range(CH):
                        if c == 0 and CH - 1 in LOW_DVE:
                            p_low(PAIRS * n + slot, slot, CH - 1)
                        if c == 0 and not (last and slot + 2 >= PAIRS):
                            max_rows(n, slot + 2)
                        if c == 0 and not (first and slot == 0):
                            y_norm(PAIRS * n + slot - 1, slot - 1, 1)
                        if c == 4:
                            y_norm(PAIRS * n + slot, slot, 0)
                        if not (last and slot + 3 >= PAIRS):
                            maxes(PAIRS * n + slot + 3, slot + 3, c)
                        if c - 1 in LOW_DVE and not (last and slot + 1 >= PAIRS):
                            p_low(PAIRS * n + slot + 1, slot + 1, c - 1)
                        for job in table[slot, c]:
                            before = None
                            if job[:2] == ("O", 1):
                                before = at["O", 0] + 1
                            if job[:2] == ("O", -1):
                                before = o_before(job_base(n, False), False) + 1
                            read(n, *job, before=before)

            def epilogue():
                y_norm(PAIRS * NB - 1, PAIRS - 1, 1)
                jobs = numbered_epilogue()
                for job in jobs:
                    read(NB, *job, before=o_before(jobs[0][2], True) + 1)

            batches(dve, prologue, body, epilogue)

        @block.tensor
        def _(pe):
            def mm(o, l, r, start, stop):
                return nc.tensor.matmul(o, l, r, start=start, stop=stop)

            def three(o, lh, ll, rh, rl, start, stop):
                mm(o, lh, rh, start, False)
                mm(o, lh, rl, False, False)
                return mm(o, ll, rh, False, stop)

            def job(n, first, kind, which, k, h, bank, x_read=None, y_read=None, o_read=None):
                dst = job_bank[bank]
                if positive(k - 1):
                    pe.wait_ge(job_read, k - 1)
                if kind == "X":
                    pe.wait_ge(xn_done, (n + 1) * TT)
                    for i in range(TT):
                        last = nc.tensor.transpose(dst[:, i * P:(i + 1) * P], xn[:, i, :], id32[:, :])
                elif kind in "QK":
                    if x_read is not None:
                        pe.wait_ge(job_read, x_read)
                    w, s = int(kind == "K"), slice((which % PAIRS) * P, (which % PAIRS) * P + P)
                    last = three(dst[:, :], w_hi[:, w, s], w_lo[:, w, s], xT_hi[:, :], xT_lo[:, :], True, True)
                elif kind == "V":
                    q, half = (which // 2) % QUADS, which % 2
                    s = slice(q * 256, (q + 1) * 256)
                    for j in range(2):
                        t = slice((2 * half + j) * P, (2 * half + j + 1) * P)
                        last = three(dst[:, j * 256:(j + 1) * 256], xT_hi[:, t], xT_lo[:, t], w_hi[:, 2, s], w_lo[:, 2, s], True, True)
                elif kind == "F":
                    for half in range(2):
                        t = slice(half * HALF, (half + 1) * HALF)
                        last = three(dst[half * M:(half + 1) * M, 0:HALF], win_hi[:, :], win_lo[:, :], xT_hi[:, t], xT_lo[:, t], True, True)
                elif kind == "Y":
                    g = PAIRS * n + which
                    pe.wait_ge(y_lo_done, g + 1)
                    d16 = dst[:, :].bitcast(f16)
                    for a, part in enumerate((y_hi, y_lo)):
                        for i in range(TT):
                            at = (a * TT + i) * P
                            last = nc.tensor.transpose(d16[:, at:at + P], part[:, which % 2, i, :], id16[:, :])
                        if a == 0:
                            last.then_inc(yt_done, 1)
                elif kind == "O":
                    pairs = O_PAIRS[which]
                    pe.wait_ge(job_read, y_read)
                    for p in pairs:
                        s = slice(p * C, (p + 1) * C)
                        last = three(dst[:, :], w_hi[:, 3, s], w_lo[:, 3, s], yT[:, p, 0, :], yT[:, p, 1, :],
                                     p == pairs[0], which >= 0 and p == pairs[-1])
                    if which < 0:
                        pe.wait_ge(ffn_step, FFN_STEPS * n)
                        pe.wait_ge(w_hi_done, 7)
                        for half in range(2):
                            last = mm(dst[:, half * HALF:(half + 1) * HALF], wout[:, half, :], fg[:, :], False, half == 1)
                elif kind == "R":
                    pe.wait_ge(job_read, o_read)
                    for i in range(TT):
                        last = nc.tensor.transpose(dst[:, i * P:(i + 1) * P], oT[:, i * P:(i + 1) * P], id32[:, :])
                last.then_inc(job_done, 1)

            def approx(n, p, c):
                g = PAIRS * n + p
                if c == 0:
                    pe.wait_ge(stacked[p % SB], 96 * uses(n, p))
                if positive(CH * g + c - 1):
                    pe.wait_ge(max_done, CH * g + c - 1)
                if c == 1 and positive(g):
                    pe.wait_ge(mrow_done, g)
                dst, s4, at = approx_bank[(CH * p + c) % 2], p % SB, 0
                for h, j in PARTS[c]:
                    i = TT - 1 - j
                    w = (i + 1) * P
                    mm(dst[:, at:at + w], stack[:, s4, Q_ST, h, i * P:(i + 1) * P], stack[:, s4, K_ST, h, 0:w], True, False)
                    last = mm(dst[:, at + i * P:at + w], idb[:, :], maskb[:, :], False, True)
                    at += w
                last.then_inc(approx_done, 1)

            def turn_maxima(g, p):
                pe.wait_ge(mx16_done, g + 1)
                nc.tensor.transpose(turned_to(p), mx16[:, p % 2, :], id16[:, :]).then_inc(turned, 1)

            def scores(n, p, c):
                g = PAIRS * n + p
                if c == 0:
                    pe.wait_ge(mrow_in[p % SB], 16 * uses(n, p))
                if positive(CH * g + c - 1):
                    pe.wait_ge(exp_done, CH * g + c - 1)
                dst, s4, at = score_bank[(CH * p + c) % 2], p % SB, 0
                for h, j in PARTS[c]:
                    w, s, t = T - j * P, slice(j * P, (j + 1) * P), slice(j * P, T)
                    mm(dst[:, at:at + w], stack[:, s4, K_ST, h, s], stack[:, s4, Q_ST, h, t], True, False)
                    mm(dst[:, at:at + P], idb[:, :], maskT[:, :], False, False)
                    last = mm(dst[:, at:at + w], stack[0:D + 1, s4, K_MX, h, s], stack[0:D + 1, s4, Q_MX, h, t], False, True)
                    at += w
                last.then_inc(score_done, 1)

            BLOCKS = [(h, i, j) for rows in ((0, 1), (2, 3)) for h in range(2) for i in rows for j in range(i + 1)]

            SIZES = (3, 4, 5, 4, 4)
            assert sum(SIZES) == len(BLOCKS)

            def pv(n, first, g, p, part):
                if part == 0:
                    for c in (0, 2):
                        pe.wait_ge(*low_there(g, c))
                    pe.wait_ge(job_read, v_jobs_done(n, first, p))
                if part == 1:
                    for c in (3, 4):
                        pe.wait_ge(*low_there(g, c))
                q, b = p // 2, p % 2
                for h, i, j in BLOCKS[sum(SIZES[:part]):sum(SIZES[:part + 1])]:
                    if i == 0 and positive(2 * g + h - 1):
                        pe.wait_ge(y32_done, 2 * g + h - 1)
                    hh = (p % 2) * 2 + h
                    s = slice(col(h, j) + (i - j) * P, col(h, j) + (i - j + 1) * P)
                    o = y_bank[h][:, i * VW:i * VW + VW]
                    mm(o, p_hi[:, b, s], v_hi[:, q, j, hh, :], j == 0, False)
                    mm(o[:, 0:D], p_hi[:, b, s], v_lo[:, q, j, hh, :], False, False)
                    last = mm(o, p_lo[:, b, s], v_hi[:, q, j, hh, :], False, j == i)
                    if (i, j) == (TT - 1, TT - 1):
                        last.then_inc(pv_done, 1)

            def prologue():
                jobs = numbered_prologue()
                pe.wait_ge(consts, 10)
                for j in jobs:
                    if j[:2] == ("Q", 0):
                        pe.wait_ge(w_lo_done, 2)
                    if j[:2] == ("V", 0):
                        pe.wait_ge(w_lo_done, 5)
                    job(0, True, *j, x_read=1 if j[:2] == ("Q", 0) else None)
                    if j[:2] == ("V", 1):
                        pe.wait_ge(consts, 13)
                        for c in range(2):
                            scores(0, 0, c)
                    if j[:2] in APPROX_MADE:
                        p = APPROX_MADE.index(j[:2])
                        for c in range(CH):
                            approx(0, p, c)
                        if p < 2:
                            turn_maxima(p, p)
                for c in range(2, CH):
                    scores(0, 0, c)

            def body(n, first, last):
                table = numbered(n, first, last)
                at = {(kind, which): k for row in table.values() for kind, which, k, _, _ in row}
                for slot in range(PAIRS):
                    for c in range(CH):
                        if not (last and slot + 1 >= PAIRS):
                            scores(n, slot + 1, c)
                        for j in table[slot, c]:
                            job(n + 1 if j[0] == "X" else n, first, *j,
                                x_read=at["X", 0] + 1 if j[:2] == ("Q", PAIRS) else None,
                                y_read=at["Y", O_PAIRS[j[1]][-1] - PAIRS * (j[1] < 0)] + 1 if j[0] == "O" else None,
                                o_read=at["O", -1] + 1 if j[0] == "R" else None)
                        if not (last and slot + 3 >= PAIRS):
                            approx(n, slot + 3, c)
                        if c == 0 and not (last and slot + 2 >= PAIRS):
                            turn_maxima(PAIRS * n + slot + 2, slot + 2)
                        pv(n, first, PAIRS * n + slot, slot, c)

            def epilogue():
                for j in numbered_epilogue():
                    job(NB - 1 if j[0] == "Y" else NB, False, *j, y_read=j[2], o_read=j[2])

            batches(pe, prologue, body, epilogue)


_INS = ["x", "wqT", "wkT", "wvT", "wo", "w_in", "b_in", "w1", "b1", "w2", "b2", "w_out", "b_out"]


def kernel(L0_attn_x, L0_attn_w_q, L0_attn_w_k, L0_attn_w_v, L0_attn_w_o, L0_ffn_Win, L0_ffn_bin_, L0_ffn_W1,
           L0_ffn_b1, L0_ffn_W2, L0_ffn_b2, L0_ffn_Wout, L0_ffn_bout):
    import concourse.bacc as bacc
    from concourse import mybir as mb
    from concourse.bass_utils import run_bass_kernel_spmd

    def rows_to_columns(w):
        w = np.asarray(w)
        return np.ascontiguousarray(w.reshape(-1, w.shape[-1]).T)

    given = [np.asarray(L0_attn_x), rows_to_columns(L0_attn_w_q), rows_to_columns(L0_attn_w_k), rows_to_columns(L0_attn_w_v),
             np.asarray(L0_attn_w_o), np.asarray(L0_ffn_Win), np.asarray(L0_ffn_bin_), np.asarray(L0_ffn_W1),
             np.asarray(L0_ffn_b1), np.asarray(L0_ffn_W2), np.asarray(L0_ffn_b2), np.asarray(L0_ffn_Wout), np.asarray(L0_ffn_bout)]
    nc = bacc.Bacc("TRN2", target_bir_lowering=False, num_devices=1)
    arrays, args = {}, []
    for name, a in zip(_INS, given):
        a = np.ascontiguousarray(a)
        arrays[name + "_dram"] = a
        args.append(nc.dram_tensor(name + "_dram", a.shape, mb.dt.from_np(a.dtype), kind="ExternalInput").ap())
    out = nc.dram_tensor("out_dram", given[0].shape, mb.dt.float32, kind="ExternalOutput").ap()
    transformer_block(nc, *args, out)
    r = run_bass_kernel_spmd(nc, [arrays], core_ids=[0])
    return r.results[0]["out_dram"]
```
